# Optimizing a Trainium2 kernel written in Bass

```python
import numpy as np
import jax
import jax.numpy as jnp

def _softmax(x, axis=-1):
    return jax.nn.softmax(x, axis=axis)

def _gelu(x):
    return jax.nn.gelu(x, approximate=True)

def _silu(x):
    return jax.nn.silu(x)

def _sigmoid(x):
    return jax.nn.sigmoid(x)

def _layernorm(x, axis=-1, eps=1e-05):
    m = jnp.mean(x, axis=axis, keepdims=True)
    v = jnp.var(x, axis=axis, keepdims=True)
    return (x - m) / jnp.sqrt(v + eps)

def _scatter_add(tgt, idx, src, axis=0):
    return tgt.at[idx].add(src)

def _segment_sum(src, seg, n):
    return jax.ops.segment_sum(src, seg, n)
kernel_name = 'mk_adj_resnorm_d1_adj_r2_59599d'

def setup_inputs(seed: int=0):
    np.random.seed(seed)
    _w = jnp.asarray

    def _rec_inputs():
        import jax
        import jax.numpy as jnp
        _gk = jax.random.key(seed)
        x = -0.0002928 + 1 * jax.random.normal(jax.random.fold_in(_gk, 1), (4096, 256), jnp.float32)
        _a = jax.random.bernoulli(jax.random.fold_in(_gk, 2), 0.000488281, (4096, 4096))
        adj = _a.astype(jnp.int32)
        return (x, adj)
    x, adj = _rec_inputs()

    def _L0_gnn_setup():
        import jax, jax.numpy as jnp
        import numpy as np
        EPS = 1e-08
        key = jax.random.key(seed)
        k1, k2, k3 = jax.random.split(key, 3)
        N, IN_DIM, OUT_DIM = (4096, 256, 256)
        h = jax.random.normal(k1, (N, IN_DIM), dtype=jnp.float32)
        adj = jax.random.randint(k2, (N, N), 0, 2, dtype=jnp.int32)
        W = jax.random.normal(k3, (OUT_DIM, IN_DIM), dtype=jnp.float32) * (1.0 / np.sqrt(IN_DIM))
        return {'h': h, 'adj': adj, 'W': W}
    _L0_gnn_all = _L0_gnn_setup()
    _L0_gnn_in = {k: v for k, v in _L0_gnn_all.items() if k in ('W',)}
    del _L0_gnn_all
    return {'x': x, 'adj': adj, 'L0_gnn_W': _L0_gnn_in['W']}

def reference(x, adj, L0_gnn_W):
    import jax
    import jax.numpy as jnp

    def _L0_gnn_ref(h, adj, W):
        import jax, jax.numpy as jnp
        import numpy as np
        EPS = 1e-08
        Wh = h @ W.T
        N = Wh.shape[0]
        norms = jnp.linalg.norm(Wh, axis=1, keepdims=True)
        sim = Wh @ Wh.T / (norms * norms.T + EPS)
        mask = (adj > 0) | jnp.eye(N, dtype=bool)
        sim_masked = jnp.where(mask, sim, -jnp.inf)
        alpha = jax.nn.softmax(sim_masked, axis=1)
        return alpha @ Wh
    x = _layernorm(x + _L0_gnn_ref(x, adj, L0_gnn_W), axis=-1)
    return x

_drawn_inputs = setup_inputs


def setup_inputs(seed=0):
    import zlib

    import numpy as np

    out = dict(_drawn_inputs(seed))
    spreads = {}
    factors = {}
    for name, (base, spread) in spreads.items():
        noise = np.random.default_rng([zlib.crc32(name.encode()), seed]).standard_normal(out[name].shape)
        drawn = base * np.exp(spread * noise) if base else spread * noise
        out[name] = jnp.asarray(drawn.astype(out[name].dtype))
    for name, factor in factors.items():
        out[name] = (out[name] * factor).astype(out[name].dtype)
    return out
```

```python
from contextlib import ExitStack

import concourse.bass as bass
from concourse import mybir

ALU = mybir.AluOpType
ACT = mybir.ActivationFunctionType
F32 = mybir.dt.float32
BF16 = mybir.dt.bfloat16
I32 = mybir.dt.int32
P = 128
SIM_EPS = 1e-8
LN_EPS = 1e-5


def gnn_layer(nc, x, adj, w, out):
    N, D = x.shape
    T = N // P
    K = D // P
    CH = 512
    NC_ = N // CH
    B = CH // P
    x_t = x.rearrange("(t p) d -> p t d", p=P)
    adj_t = adj.rearrange("(t p) j -> p t j", p=P)
    out_t = out.rearrange("(t p) d -> p t d", p=P)
    w_h = w.rearrange("(h p) d -> p h d", p=P)

    with ExitStack() as ctx:
        def sb(name, shape, dt=F32):
            return ctx.enter_context(nc.sbuf_tensor(name, shape, dt))

        def ps(name, shape, dt=F32):
            return ctx.enter_context(nc.psum_tensor(name, shape, dt))

        def sem(name):
            return ctx.enter_context(nc.semaphore(name))

        X = sb("X", [P, T, D])
        Wh = sb("Wh", [P, T, D + 2])
        xs = sb("xs", [P, 2, D])
        wsb = sb("wsb", [P, K, D])
        WT = sb("WT", [P, K, D])
        xT = sb("xT", [P, 2, D])
        nsq = sb("nsq", [P, T])
        ident = sb("ident", [P, P])
        ones = sb("ones", [P, P])
        junk = sb("junk", [P, 2, D])
        eps = sb("eps", [P, 1])
        WhT = sb("WhT", [P, K, N])
        nrow = sb("nrow", [P, N])
        diag = sb("diag", [P, P])
        adjr = sb("adjr", [P, N], I32)
        lw = sb("lw", [P, K, P])
        den = sb("den", [P, CH])
        rec = sb("rec", [P, CH])
        sim = sb("sim", [P, CH])
        ex = sb("ex", [P, CH])
        pr = sb("pr", [P, CH])
        pT = sb("pT", [P, B, P])
        y = sb("y", [P, D + 1])
        z = sb("z", [P, D])
        st = sb("st", [P, 6])
        mv = sb("mv", [P, 2])
        sm = sb("sm", [P, 4])
        yo = sb("yo", [P, D])

        bank = [ps(f"bank{i}", [P, CH]) for i in range(8)]

        names = ("w_loaded const_done x_kept0 x_kept1 xT_free0 xT_free1 x_turned xT_ready xTsb_free0 xTsb_free1 "
                 "wh_free0 wh_free1 wh_done wh_kept w_turned w_ready norm_sem x_loaded0 x_loaded1").split()
        S = {n: sem(n) for n in names}
        adj_loaded = sem("adj_loaded")
        stored = sem("stored")
        t_ps = sem("t_ps")
        t_sb = sem("t_sb")
        n_dg = sem("n_dg")
        n_ps = sem("n_ps")
        n_sb = sem("n_sb")
        passed = sem("passed")
        (tile_free, lw_ready, s_ps, den_ok, rec_ok, sim_ready, ex_ready, diag_ok, p_ready, pT_ps, pT_ready, pv_done, fin, y_ready,
         lnv, rstd) = [sem(n) for n in "tile_free lw_ready s_ps den_ok rec_ok sim_ready ex_ready diag_ok p_ready pT_ps pT_ready pv_done fin y_ready lnv rstd".split()]

        block = ctx.enter_context(nc.Block())

        @block.sync
        def _(sp):
            sp.dma_start(wsb[:], w_h).then_inc(S["w_loaded"], 16)
            for b in range(2):
                sp.dma_start(xs[:, b, :], x_t[:, b, :]).then_inc(S[f"x_loaded{b}"], 16)
            with sp.Fori(1, T // 2) as g:
                for b in range(2):
                    sp.wait_ge(S["x_turned"], 2 * g + b - 1)
                    sp.wait_ge(S[f"x_kept{b}"], g)
                    sp.dma_start(xs[:, b, :], x_t[:, bass.ds(2 * g + b, 1), :]).then_inc(S[f"x_loaded{b}"], 16)
            with sp.Fori(0, T) as t:
                sp.dma_start(adjr[:], adj_t[:, bass.ds(t, 1), :]).then_inc(adj_loaded, 16)
                sp.wait_ge(y_ready, t + 1)
                sp.dma_start(out_t[:, bass.ds(t, 1), :], yo[:]).then_inc(stored, 16)
                sp.wait_ge(stored, t * 16 + 16)
                sp.sem_inc(tile_free, 1)

        @block.gpsimd
        def _(pool):
            pool.memset(ones[:], 1.0)
            pool.memset(eps[:], LN_EPS)
            pool.memset(Wh[:, :, D:D + 1], 1.0)
            pool.memset(ident[:], 0.0).then_inc(S["norm_sem"], 1)
            pool.wait_ge(S["norm_sem"], 1)
            pool.affine_select(out=ident[:], in_=ident[:], compare_op=ALU.not_equal, fill=1.0, base=0,
                               pattern=[[-1, P]], channel_multiplier=1).then_inc(S["const_done"], 1)
            with pool.Fori(0, T // 2) as g:
                for b in range(2):
                    pool.wait_ge(S[f"x_loaded{b}"], 16 * g + 16)
                    pool.tensor_copy(X[:, bass.ds(2 * g + b, 1), :], xs[:, b, :]).then_inc(S[f"x_kept{b}"], 1)

        @block.tensor
        def _(pe):
            pe.wait_ge(S["const_done"], 1)
            pe.wait_ge(S["w_loaded"], 16)
            for h in range(K):
                for k in range(K):
                    last = pe.transpose(bank[4][:, k * D + h * P:k * D + h * P + P], wsb[:, h, k * P:k * P + P], ident[:])
            last.then_inc(S["w_turned"], 1)
            pe.wait_ge(S["w_ready"], 1)
            with pe.Fori(0, T // 2) as g:
                for b in range(2):
                    pe.wait_ge(S[f"x_loaded{b}"], 16 * g + 16)
                    pe.wait_ge(S[f"xT_free{b}"], g + 1)
                    for k in range(K):
                        last = pe.transpose(bank[b][:, k * P:k * P + P], xs[:, b, k * P:k * P + P], ident[:])
                    last.then_inc(S["x_turned"], 1)
                for b in range(2):
                    pe.wait_ge(S["xT_ready"], 2 * g + b + 1)
                    pe.wait_ge(S[f"wh_free{b}"], g + 1)
                    for k in range(K):
                        last = pe.matmul(bank[2 + b][:, 0:D], xT[:, b, k * P:k * P + P], WT[:, k, :],
                                         start=k == 0, stop=k == K - 1)
                    last.then_inc(S["wh_done"], 1)
            with pe.Fori(0, T) as t:
                pe.wait_ge(t_sb, 2 * t + 1)
                for k in range(K):
                    last = pe.transpose(bank[0][:, k * P:k * P + P], lw[:, k, :], ident[:])
                last.then_inc(t_ps, 1)
                pe.wait_ge(n_dg, t + 1)
                pe.wait_ge(n_sb, t + 1)
                pe.matmul(bank[1][:, 0:P], ones[:], diag[:], start=True, stop=True).then_inc(n_ps, 1)
            with pe.Fori(0, T) as t:
                q = t * NC_
                pe.wait_ge(lw_ready, t + 1)
                for c in range(NC_):
                    if c >= 1:
                        pe.wait_ge(sim_ready, q + c)
                    for k in range(K):
                        last = pe.matmul(bank[2][:], lw[:, k, :], WhT[:, k, c * CH:c * CH + CH], start=k == 0, stop=k == K - 1)
                    last.then_inc(s_ps, 1)
                    pe.wait_ge(p_ready, q + c + 1)
                    if c >= 1:
                        pe.wait_ge(pT_ready, q + c)
                    for b in range(B):
                        last = pe.transpose(bank[3][:, b * P:b * P + P], pr[:, b * P:b * P + P], ident[:])
                    last.then_inc(pT_ps, 1)
                    pe.wait_ge(pT_ready, q + c + 1)
                    for b in range(B):
                        last = pe.matmul(bank[4][:, 0:D + 1], pT[:, b, :], Wh[:, c * B + b, 0:D + 1],
                                         start=c == 0 and b == 0, stop=c == NC_ - 1 and b == B - 1)
                    last.then_inc(pv_done, 1)

        @block.scalar
        def _(act):
            act.sem_inc(S["xT_free0"], 1)
            act.sem_inc(S["xT_free1"], 1)
            act.sem_inc(S["wh_free0"], 1)
            act.sem_inc(S["wh_free1"], 1)
            act.wait_ge(S["w_turned"], 1)
            act.activation(WT[:], bank[4][:].rearrange("p (k d) -> p k d", k=K), ACT.Copy).then_inc(S["w_ready"], 1)
            with act.Fori(0, T // 2) as g:
                for b in range(2):
                    act.wait_ge(S["x_turned"], 2 * g + b + 1)
                    act.wait_ge(S["wh_done"], 2 * g + b + 1 - 2) if 0 else None
                    act.activation(xT[:, b, :], bank[b][:, 0:D], ACT.Copy).then_inc(S["xT_ready"], 1)
                    act.wait_ge(S["xT_ready"], 2 * g + b + 1)
                    act.sem_inc(S[f"xT_free{b}"], 1)
                for b in range(2):
                    t = 2 * g + b
                    act.wait_ge(S["wh_done"], t + 1)
                    act.activation(Wh[:, bass.ds(t, 1), 0:D], bank[2 + b][:, 0:D], ACT.Copy)
                    act.activation(junk[:, b, :], bank[2 + b][:, 0:D], ACT.Square,
                                   accum_out=nsq[:, bass.ds(t, 1)]).then_inc(S["wh_kept"], 1)
                    act.wait_ge(S["wh_kept"], 2 * t + 1)
                    act.sem_inc(S[f"wh_free{b}"], 1)
                    act.activation(Wh[:, bass.ds(t, 1), D + 1:D + 2], nsq[:, bass.ds(t, 1)], ACT.Sqrt).then_inc(S["wh_kept"], 1)
            act.wait_ge(S["wh_kept"], 2 * T)
            with act.Fori(0, T) as t:
                act.activation(lw[:], Wh[:, bass.ds(t, 1), 0:D].rearrange("p a (k c) -> p (a k) c", k=K), ACT.Copy).then_inc(t_sb, 1)
                act.wait_ge(t_ps, t + 1)
                act.activation(WhT[:, :, bass.ds(t * P, P)], bank[0][:, 0:D].rearrange("p (k c) -> p k c", k=K), ACT.Copy).then_inc(t_sb, 1)
                act.wait_ge(t_sb, 2 * t + 2)
            act.sem_inc(tile_free, 1)
            with act.Fori(0, T) as t:
                q = t * NC_
                act.wait_ge(tile_free, t + 1)
                act.activation(lw[:], WhT[:, :, bass.ds(t * P, P)], ACT.Copy).then_inc(lw_ready, 1)
                for c in range(NC_):
                    act.wait_ge(sim_ready, q + c + 1)
                    if c >= 1:
                        act.wait_ge(p_ready, q + c)
                    act.activation(ex[:], sim[:], ACT.Exp).then_inc(ex_ready, 1)
                    act.wait_ge(pT_ps, q + c + 1)
                    if c >= 1:
                        act.wait_ge(pv_done, q + c)
                    act.activation(pT[:], bank[3][:].rearrange("p (b c) -> p b c", b=B), ACT.Copy).then_inc(pT_ready, 1)
                act.wait_ge(fin, 6 * t + 5)
                act.activation(sm[:, 0:1], mv[:, 1:2], ACT.Ln, bias=eps[:, 0:1]).then_inc(lnv, 1)
                act.wait_ge(lnv, t + 1)
                act.activation(sm[:, 1:2], sm[:, 0:1], ACT.Exp, scale=-0.5).then_inc(rstd, 1)
                act.wait_ge(fin, 6 * t + 6)
                act.activation(yo[:], z[:], ACT.Identity, scale=sm[:, 1:2], bias=sm[:, 2:3]).then_inc(y_ready, 1)

        @block.vector
        def _(dve):
            dve.wait_ge(S["const_done"], 1)
            dve.wait_ge(S["wh_kept"], 2 * T)
            dve.sem_inc(n_sb, 1)
            with dve.Fori(0, T) as t:
                dve.tensor_scalar(diag[:], ident[:], Wh[:, bass.ds(t, 1), D + 1:D + 2].rearrange("p a b -> p (a b)"),
                                  None, ALU.mult).then_inc(n_dg, 1)
                dve.wait_ge(n_ps, t + 1)
                dve.tensor_copy(nrow[:, bass.ds(t * P, P)], bank[1][:, 0:P]).then_inc(n_sb, 1)
            dve.wait_ge(n_sb, T + 1)
            dve.wait_ge(t_sb, 2 * T)
            for b in range(2):
                dve.wait_ge(S[f"x_kept{b}"], T // 2)
            with dve.Fori(0, T) as t:
                q = t * NC_
                ni = Wh[:, bass.ds(t, 1), D + 1:D + 2].rearrange("p a b -> p (a b)")
                blk = adjr[:, bass.ds(t * P, P)]
                dve.wait_ge(tile_free, t + 1)
                dve.wait_ge(adj_loaded, 16 * t + 16)
                dve.tensor_tensor(blk, blk, ident[:], ALU.max).then_inc(diag_ok, 1)
                dve.wait_ge(diag_ok, t + 1)
                for c in range(NC_):
                    cs = slice(c * CH, c * CH + CH)
                    if c >= 1:
                        dve.wait_ge(sim_ready, q + c)
                    dve.tensor_scalar(den[:], nrow[:, cs], ni, SIM_EPS, ALU.mult, ALU.add).then_inc(den_ok, 1)
                    dve.wait_ge(den_ok, q + c + 1)
                    dve.reciprocal(rec[:], den[:]).then_inc(rec_ok, 1)
                    dve.wait_ge(rec_ok, q + c + 1)
                    dve.wait_ge(s_ps, q + c + 1)
                    if c >= 1:
                        dve.wait_ge(ex_ready, q + c)
                    dve.tensor_tensor(sim[:], bank[2][:], rec[:], ALU.mult).then_inc(sim_ready, 1)
                    dve.wait_ge(ex_ready, q + c + 1)
                    if c >= 1:
                        dve.wait_ge(pT_ps, q + c)
                    dve.scalar_tensor_tensor(out=pr[:], in0=adjr[:, cs], scalar=0.0, in1=ex[:], op0=ALU.is_gt,
                                             op1=ALU.mult).then_inc(p_ready, 1)
                e = 6 * t
                dve.wait_ge(pv_done, q + NC_)
                dve.reciprocal(sm[:, 3:4], bank[4][:, D:D + 1]).then_inc(fin, 1)
                dve.wait_ge(fin, e + 1)
                dve.tensor_scalar(y[:, 0:D], bank[4][:, 0:D], sm[:, 3:4], None, ALU.mult).then_inc(fin, 1)
                dve.wait_ge(fin, e + 2)
                dve.tensor_tensor(z[:], y[:, 0:D], X[:, bass.ds(t, 1), :].rearrange("p a b -> p (a b)"), ALU.add).then_inc(fin, 1)
                dve.wait_ge(fin, e + 3)
                dve.bn_stats(st[:], z[:]).then_inc(fin, 1)
                dve.wait_ge(fin, e + 4)
                dve.sem_inc(passed, 1)
                dve.bn_aggr(mv[:], st[:]).then_inc(fin, 1)
                dve.wait_ge(fin, e + 5)
                dve.wait_ge(rstd, t + 1)
                dve.scalar_tensor_tensor(out=sm[:, 2:3], in0=mv[:, 0:1], scalar=-1.0, in1=sm[:, 1:2],
                                         op0=ALU.mult, op1=ALU.mult).then_inc(fin, 1)


_INS = ["x", "adj", "L0_gnn_W"]


def kernel(**inputs):
    import numpy as _np
    import concourse.bacc as _bacc
    from concourse import mybir as _mybir
    from concourse.bass_utils import run_bass_kernel_spmd as _run

    nc = _bacc.Bacc("TRN2", target_bir_lowering=False, num_devices=1)
    arrays, args = {}, []
    for name in _INS:
        a = _np.ascontiguousarray(inputs[name])
        arrays[f"in_{name}"] = a
        args.append(nc.dram_tensor(f"in_{name}", a.shape, _mybir.dt.from_np(a.dtype), kind="ExternalInput").ap())
    o = nc.dram_tensor("out_0", inputs["x"].shape, _mybir.dt.float32, kind="ExternalOutput").ap()
    gnn_layer(nc, *args, o)
    r = _run(nc, [arrays], core_ids=[0])
    return r.results[0]["out_0"]
```

```python
from contextlib import ExitStack

import concourse.bass as bass
from concourse import mybir

ALU = mybir.AluOpType
ACT = mybir.ActivationFunctionType
AX = mybir.AxisListType
F32 = mybir.dt.float32
F16 = mybir.dt.float16
BF16 = mybir.dt.bfloat16
I32 = mybir.dt.int32
U32 = mybir.dt.uint32
P = 128
SIM_EPS = 1e-8
LN_EPS = 1e-5
TINY = 1e-30

WORDS = 256
BITS = 16
LO = 256.0
EXP_BITS = 0x7F800000
J_SHIFT = 256 * (127 + 8) - 255
K1 = 16
SLOTS = 16
KEYS = 3 * K1
LEFT = KEYS
LIST = 2 * LEFT - K1 - 6
OV_STEP = LEFT - K1 + 1
EC = 3
EDGES = EC * P
INFO = 20
I_OFF, I_NORM, I_ROW, I_END = 16, 17, 18, 19
NT = 4
Q_ACT = 15
GATHER, DOT, SUM, NORM, OUT = 1, 3, 4, 5, 6


def wait(eng, s, v):
    if not isinstance(v, int) or v > 0:
        eng.wait_ge(s, v)


def gnn_layer(nc, x, adj, w, out, force_dense=False):
    N, D = x.shape
    T = N // P
    K = D // P
    NB = T // NT
    XC = 4
    XPAIRS = T // XC // 2
    LATE = T // 2 - 2 * NT
    XT = T // XC
    ROW = D + 2
    x_t = x.rearrange("(t p) d -> p t d", p=P)
    adj_t = adj.rearrange("(t p) j -> p t j", p=P)
    out_t = out.rearrange("(t p) d -> p t d", p=P)
    w_h = w.rearrange("(h p) d -> p h d", p=P)
    wh_rows = nc.dram_tensor("wh_rows", (N, ROW), F32, kind="Internal").ap()
    wh_rows_t = wh_rows.rearrange("(t p) d -> p t d", p=P)

    with ExitStack() as ctx:
        def sb(name, shape, dt=F32):
            return ctx.enter_context(nc.sbuf_tensor(name, shape, dt))

        def ps(name, shape, dt=F32):
            return ctx.enter_context(nc.psum_tensor(name, shape, dt))

        def sem(name):
            return ctx.enter_context(nc.semaphore(name))

        ident = sb("ident", [P, P])
        ones = sb("ones", [P, P])
        tri = sb("tri", [P, P])
        bit_w = sb("bit_w", [P, BITS, P], BF16)
        bias_rows = sb("bias_rows", [P, WORDS], BF16)
        ones_b = sb("ones_b", [P, P], BF16)
        edge_no = sb("edge_no", [P, EDGES], F16)
        edge_of = sb("edge_of", [P, EC])
        slot_no = sb("slot_no", [P, EC, SLOTS])
        row1_no = sb("row1_no", [P, P])
        iota_i = sb("iota_i", [P, EDGES], I32)
        ln_eps = sb("ln_eps", [P, 1])
        neg_half = sb("neg_half", [P, 1])
        X = sb("X", [P, T, D])
        Wh = sb("Wh", [P, T, ROW])
        nsq = sb("nsq", [P, T])
        adj_d = sb("adj_d", [P, T], I32)
        wself = sb("wself", [P, T])
        self_t = sb("self_t", [P, T])
        xs = sb("xs", [P, 2, D])
        wsb = sb("wsb", [P, K, D])
        WT = sb("WT", [P, K, D])
        xT = sb("xT", [P, 2, D])
        junk = sb("junk", [P, EC, D])
        junk_a = sb("junk_a", [P, 2, D])
        adjb = sb("adjb", [P, NT, N], I32)
        mask = sb("mask", [P, 2, N], BF16)
        keys_left = sb("keys_left", [P, WORDS])
        KK = sb("KK", [P, NT, LIST + SLOTS])
        key_i = sb("key_i", [P, NT, K1], I32)
        key_e = sb("key_e", [P, NT, K1], I32)
        key_p = sb("key_p", [P, NT, K1], I32)
        key_r = sb("key_r", [P, NT, K1])
        V_left = sb("V_left", [P, NT, KEYS])
        valid = sb("valid", [P, NT, SLOTS])
        cnt = sb("cnt", [P, NT])
        info = sb("info", [P, NT, INFO])
        ov_k = sb("ov_k", [P, NT, 3])
        ov_e = sb("ov_e", [P, NT])
        ge = sb("ge", [P, EDGES], F16)
        R = sb("R", [P, 4, EDGES])
        slot_e = sb("slot_e", [P, EC])
        hit = sb("hit", [P, EC, SLOTS])
        hitj = sb("hitj", [P, EC, SLOTS])
        jf = sb("jf", [P, EC])
        J = sb("J", [P, 4, EC], I32)
        einfo = sb("einfo", [P, 4, EC, INFO])
        G = sb("G", [P, 4, EC, ROW])
        dot = sb("dot", [P, EC])
        nn = sb("nn", [P, EC])
        sim = sb("sim", [P, 2, EC])
        we = sb("we", [P, 2, EC])
        O = sb("O", [P, 2, EC, P])
        dself = sb("dself", [P, 2, P])
        rinv = sb("rinv", [P, 2])
        ysb = sb("ysb", [P, 2, D])
        z = sb("z", [P, 2, D])
        st = sb("st", [P, 6])
        mv = sb("mv", [P, 2, 2])
        lnv = sb("lnv", [P, 2])
        rstd = sb("rstd", [P, 2])
        shift = sb("shift", [P, 2])
        yo = sb("yo", [P, 2, D])
        flag_f = sb("flag_f", [P, 4])
        flag = sb("flag", [P, 1], I32)

        pack_ps = [ps(f"pack_ps{i}", [P, 512]) for i in range(2)]
        a_ps = [ps(f"a_ps{i}", [P, 512]) for i in range(2)]
        out_ps = [ps(f"out_ps{i}", [P, 512]) for i in range(2)]
        info_bank = ps("info_bank", [P, 512])
        off_bank = ps("off_bank", [P, 512])
        off_ps = off_bank[:, 0:NT]
        info_ps = info_bank[:, 0:EC * INFO].rearrange("p (c f) -> p c f", c=EC)

        def A_chunk(c):
            return a_ps[c // 2][:, (c % 2) * D:(c % 2) * D + D]

        w_loaded = sem("w_loaded")
        diag_loaded = sem("diag_loaded")
        pool_c = sem("pool_c")
        const_done = sem("const_done")
        bits_done = sem("bits_done")
        x_loaded = [sem(f"x_loaded{q}") for q in range(XC)]
        xs_ready = sem("xs_ready")
        norm_kept = sem("norm_kept")
        x_turned = sem("x_turned")
        xT_ready = sem("xT_ready")
        wh_done = sem("wh_done")
        wh_kept = sem("wh_kept")
        rows_stored = sem("rows_stored")
        w_turned = sem("w_turned")
        w_ready = sem("w_ready")
        self_s = sem("self_s")
        self_e = sem("self_e")
        adj_loaded = [sem(f"adj_loaded{b}") for b in range(NT)]
        mask_a = sem("mask_a")
        mask_v = sem("mask_v")
        packed = sem("packed")
        find_s = sem("find_s")
        batch_s = sem("batch_s")
        cnt_ready = sem("cnt_ready")
        off_done = sem("off_done")
        info_ready = sem("info_ready")
        r_s = sem("r_s")
        info_e = sem("info_e")
        a_done = sem("a_done")
        j_s = sem("j_s")
        einfo_ready = sem("einfo_ready")
        gathered = [sem(f"gathered{b}") for b in range(4)]
        dot_s = sem("dot_s")
        we_ready = sem("we_ready")
        o_ready = sem("o_ready")
        dself_ready = sem("dself_ready")
        out_done = sem("out_done")
        rinv_ready = sem("rinv_ready")
        y_ready = sem("y_ready")
        z_ready = sem("z_ready")
        bn_s = sem("bn_s")
        ln_s = sem("ln_s")
        shift_ready = sem("shift_ready")
        yo_ready = sem("yo_ready")
        stored = [sem(f"stored{b}") for b in range(2)]
        flag_s = sem("flag_s")
        flag_ps = sem("flag_ps")
        flag_ready = sem("flag_ready")
        passed = {e: sem(f"passed_{e}") for e in ("dve", "pool", "act")}

        CH = 512
        NCH = N // CH
        B = CH // P
        adj_row = adjb[:, 0, :]
        norm_row = adjb[:, 1, :].bitcast(F32)
        WhT = adjb[:, 2:2 + K, :].bitcast(F32)
        free = mask[:].rearrange("p b n -> p (b n)").bitcast(F32)
        den, rec, sim_d, ex, pr, pT = [free[:, i * CH:i * CH + CH] for i in range(6)]
        lw = free[:, 6 * CH:6 * CH + D]
        diag = free[:, 6 * CH + D:6 * CH + D + P]
        sm = sb("sm", [P, 4])
        turn_ps, nrow_ps = pack_ps
        s_ps, pT_ps = a_ps
        pv_ps = out_ps[0]
        lw_turning = sem("lw_turning")
        lw_turned = sem("lw_turned")
        WhT_kept = sem("WhT_kept")
        diag_ready = sem("diag_ready")
        nrow_done = sem("nrow_done")
        nrow_kept = sem("nrow_kept")
        row_loaded = sem("row_loaded")
        tile_stored = sem("tile_stored")
        tile_free = sem("tile_free")
        lw_ready = sem("lw_ready")
        s_done = sem("s_done")
        den_ready = sem("den_ready")
        rec_ready = sem("rec_ready")
        sim_ready = sem("sim_ready")
        ex_ready = sem("ex_ready")
        diag_set = sem("diag_set")
        p_ready = sem("p_ready")
        pT_done = sem("pT_done")
        pT_ready = sem("pT_ready")
        pv_done = sem("pv_done")
        fin = sem("fin")
        lnv_d = sem("lnv_d")
        rstd_d = sem("rstd_d")
        out_ready = sem("out_ready")

        def overflowed(eng):
            eng.wait_ge(flag_ready, 1)
            return eng.value_load(flag[0:1, 0:1], min_val=0, max_val=1) > 0

        def wait_alone(eng, e, s, v):
            if not isinstance(v, int) or v > 0:
                eng.wait_ge(s, v)
                if not isinstance(v, int):
                    eng.sem_inc(passed[e], 1)

        block = ctx.enter_context(nc.Block())

        def slots(eng, slot):
            for n in range(2):
                for i in range(NT):
                    slot(n, i)
            with eng.Fori(2, NB - 2) as n:
                for i in range(NT):
                    slot(n, i)
            for n in range(NB - 2, NB + 2):
                for i in range(NT):
                    slot(n, i)

        def stage(n, i, d):
            t = 4 * n + (i - d)
            if isinstance(n, int) and not 0 <= t < T:
                return None
            return t

        def half(n, i, d):
            return 2 * n + (i - d) // 2

        @block.sync
        def _(sp):
            sp.dma_start(wsb[:], w_h).then_inc(w_loaded, 16)
            for q in range(XC):
                sp.dma_start(X[:, q * XT:q * XT + XT, :], x_t[:, q * XT:q * XT + XT, :]).then_inc(x_loaded[q], 16)
            for i in range(NT):
                sp.dma_start(adjb[:, i, :], adj_t[:, i, :]).then_inc(adj_loaded[i], 16)

            def slot(n, i):
                a = stage(n, i, -8)
                if a is not None:
                    wait(sp, mask_a, a - NT + 1)
                    wait(sp, mask_v, a - NT + 1)
                    sp.dma_start(adjb[:, i, :], adj_t[:, bass.ds(a, 1), :]).then_inc(adj_loaded[i], 16)
                t = stage(n, i, OUT)
                if t is not None:
                    b = (i - OUT) % 2
                    wait(sp, yo_ready, t + 1)
                    sp.dma_start(out_t[:, bass.ds(t, 1), :], yo[:, b, :]).then_inc(stored[b], 16)

            for i in range(NT):
                wait(sp, mask_a, i + 1)
                wait(sp, mask_v, i + 1)
                sp.dma_start(adjb[:, i, :], adj_t[:, NT + i, :]).then_inc(adj_loaded[i], 16)
            slots(sp, slot)
            for b in range(2):
                sp.wait_ge(stored[b], 16 * (T // 2))

            with sp.If(overflowed(sp)):
                def tile(t):
                    wait(sp, tile_free, t + 1)
                    sp.dma_start(adj_row, adj_t[:, bass.ds(t, 1), :]).then_inc(row_loaded, 16)
                    wait(sp, out_ready, t + 1)
                    sp.dma_start(out_t[:, bass.ds(t, 1), :], yo[:, 0, :]).then_inc(tile_stored, 16)
                    wait(sp, tile_stored, 16 * t + 16)
                    sp.sem_inc(tile_free, 1)

                tile(0)
                with sp.Fori(1, T) as t:
                    tile(t)

        @block.gpsimd
        def _(pool):
            pool.memset(ident[:], 0.0).then_inc(pool_c, 1)
            pool.wait_ge(pool_c, 1)
            pool.affine_select(out=ident[:], in_=ident[:], compare_op=ALU.not_equal, fill=1.0, base=0,
                               pattern=[[-1, P]], channel_multiplier=1).then_inc(const_done, 1)
            pool.memset(ones[:], 1.0)
            pool.memset(ones_b[:], 1.0)
            pool.memset(ln_eps[:], LN_EPS)
            pool.memset(neg_half[:], -0.5)
            pool.memset(Wh[:, :, D:D + 1], 1.0)
            pool.memset(tri[:], 1.0)
            pool.memset(bias_rows[:], 0.0).then_inc(pool_c, 1)
            pool.wait_ge(pool_c, 2)
            pool.affine_select(out=tri[:], in_=tri[:], compare_op=ALU.is_gt, fill=0.0, base=0,
                               pattern=[[1, P]], channel_multiplier=-1)
            pool.iota(iota_i[:, 0:WORDS], pattern=[[-1, WORDS]], base=WORDS - 1, channel_multiplier=0).then_inc(pool_c, 1)
            pool.wait_ge(pool_c, 3)
            pool.tensor_copy(bias_rows[0:1, :], iota_i[0:1, 0:WORDS]).then_inc(pool_c, 1)
            pool.wait_ge(pool_c, 4)
            pool.affine_select(out=bias_rows[:], in_=bias_rows[:], compare_op=ALU.not_equal, fill=float(2 ** 23),
                               base=-1, pattern=[[0, WORDS]], channel_multiplier=1).then_inc(pool_c, 1)
            pool.wait_ge(pool_c, 5)
            pool.affine_select(out=bias_rows[:], in_=bias_rows[:], compare_op=ALU.not_equal, fill=-128.0,
                               base=-2, pattern=[[0, WORDS]], channel_multiplier=1)
            pool.iota(iota_i[:], pattern=[[1, EDGES]], base=0, channel_multiplier=0).then_inc(pool_c, 1)
            pool.wait_ge(pool_c, 6)
            pool.tensor_copy(edge_no[:], iota_i[:])
            for c in range(EC):
                pool.tensor_copy(slot_no[:, c, 0:8], iota_i[:, 8:SLOTS])
                pool.tensor_copy(slot_no[:, c, 8:SLOTS], iota_i[:, 0:8])
            pool.tensor_copy(row1_no[:], iota_i[:, 1:P + 1]).then_inc(pool_c, 1)
            pool.wait_ge(pool_c, 7)
            pool.iota(iota_i[:, 0:EC], pattern=[[P, EC]], base=0, channel_multiplier=1).then_inc(pool_c, 1)
            pool.wait_ge(pool_c, 8)
            pool.tensor_copy(edge_of[:], iota_i[:, 0:EC]).then_inc(pool_c, 1)
            pool.wait_ge(pool_c, 9)
            pool.iota(iota_i[:, 0:1], pattern=[[0, 1]], base=1, channel_multiplier=1).then_inc(pool_c, 1)
            pool.wait_ge(pool_c, 10)
            for j in range(NT):
                last = pool.tensor_copy(info[:, j, I_ROW:I_ROW + 1], iota_i[:, 0:1])
            last.then_inc(const_done, 1)
            pool.memset(G[:], 0.0).then_inc(pool_c, 1)
            for q in range(XC):
                pool.wait_ge(norm_kept, q + 1)
                pool.dma_start(wh_rows_t[:, q * XT:q * XT + XT, :], Wh[:, q * XT:q * XT + XT, :]).then_inc(rows_stored, 16)

            pool.wait_ge(pool_c, 11)
            pool.wait_ge(rows_stored, 16 * XC)

            def slot(n, i):
                t = stage(n, i, NORM)
                if t is not None:
                    b = (i - NORM) % 2
                    wait_alone(pool, "pool", y_ready, t + 1)
                    wait_alone(pool, "pool", yo_ready, t - 1)
                    pool.tensor_tensor(z[:, b, :], ysb[:, b, :],
                                       X[:, bass.ds(t, 1), :].rearrange("p a d -> p (a d)"), ALU.add).then_inc(z_ready, 1)
                t = stage(n, i, GATHER)
                if t is not None:
                    b = (i - GATHER) % 4
                    wait_alone(pool, "pool", j_s, 5 * t + 5)
                    wait_alone(pool, "pool", out_done, t - 3)
                    for c in range(EC):
                        pool.indirect_dma_start(
                            out=G[:, b, c, :], out_offset=None, in_=wh_rows,
                            in_offset=bass.IndirectOffsetOnAxis(ap=J[:, b, c:c + 1].bitcast(U32), axis=0),
                            bounds_check=N - 1, oob_is_err=False).then_inc(gathered[b], 16)

            slots(pool, slot)

        @block.tensor
        def _(pe):
            pe.wait_ge(const_done, 1)
            pe.wait_ge(w_loaded, 16)
            for h in range(K):
                for k in range(K):
                    last = pe.transpose(info_bank[:, k * D + h * P:k * D + h * P + P], wsb[:, h, k * P:k * P + P], ident[:])
            last.then_inc(w_turned, 1)
            pe.wait_ge(w_ready, 1)

            def turn(g, b):
                wait(pe, xs_ready, 2 * g + b + 1)
                wait(pe, xT_ready, 2 * g + b - 1)
                for k in range(K):
                    last = pe.transpose(a_ps[b][:, k * P:k * P + P], xs[:, b, k * P:k * P + P], ident[:])
                last.then_inc(x_turned, 1)

            def project(g, b):
                wait(pe, xT_ready, 2 * g + b + 1)
                wait(pe, wh_kept, 2 * g + b - 1)
                for k in range(K):
                    last = pe.matmul(out_ps[b][:, 0:D], xT[:, b, k * P:k * P + P], WT[:, k, :],
                                     start=k == 0, stop=k == K - 1)
                last.then_inc(wh_done, 1)

            def turn_and_project(g):
                for b in range(2):
                    turn(g, b)
                    project(g - 1, b)

            def pack(a, j):
                b = j % 2
                wait(pe, mask_a, a + 1)
                wait(pe, mask_v, a + 1)
                wait(pe, find_s, 3 * (a - 1))
                for q in range(BITS):
                    pe.matmul(pack_ps[b][:, 0:WORDS], bit_w[:, q, :], mask[:, b, q * WORDS:q * WORDS + WORDS],
                              start=q == 0, stop=False)
                pe.matmul(pack_ps[b][:, 0:WORDS], ones_b[:], bias_rows[:], start=False, stop=True).then_inc(packed, 1)

            for b in range(2):
                turn(0, b)
            turn_and_project(1)
            with pe.Fori(2, LATE + 4) as g:
                turn_and_project(g)
            pe.wait_ge(const_done, 2)
            pe.wait_ge(bits_done, 1)
            pack(0, 0)
            for p in range(1, NT - 1):
                for g in range(2):
                    turn_and_project(LATE + 2 + 2 * p + g)
                pack(p, p)

            for b in range(2):
                project(T // 2 - 1, b)
            pack(NT - 1, NT - 1)

            def offsets(nb):
                wait(pe, cnt_ready, nb + 1)
                pe.matmul(off_ps, tri[:], cnt[:], start=True, stop=True).then_inc(off_done, 1)

            offsets(0)

            def slot(n, i):
                a = stage(n, i, -4)
                if a is not None:
                    pack(a, i)
                t = stage(n, i, DOT)
                if t is not None:
                    wait(pe, dot_s, 7 * t)
                    for c in range(EC):
                        last = pe.matmul(A_chunk(c), R[:, (i - DOT) % 4, c * P:c * P + P],
                                         Wh[:, bass.ds(t, 1), 0:D], start=True, stop=True)
                    last.then_inc(a_done, 1)
                t = stage(n, i, SUM)
                if t is not None:
                    b = (i - SUM) % 2
                    wait(pe, o_ready, t + 1)
                    wait(pe, dself_ready, t + 1)
                    wait(pe, y_ready, t - 1)
                    for c in range(EC):
                        pe.matmul(out_ps[b][:, 0:D + 1], O[:, b, c, :], G[:, (i - SUM) % 4, c, 0:D + 1],
                                  start=c == 0, stop=False)
                    pe.matmul(out_ps[b][:, 0:D + 1], dself[:, b, :], Wh[:, bass.ds(t, 1), 0:D + 1],
                              start=False, stop=True).then_inc(out_done, 1)
                t = stage(n, i, 0)
                if t is not None:
                    wait(pe, r_s, 2 * t + 2)
                    wait(pe, einfo_ready, t)
                    for c in range(EC):
                        last = pe.matmul(info_ps[:, c, :], R[:, i, c * P:c * P + P],
                                         info[:, i, :], start=True, stop=True)
                    last.then_inc(info_e, 1)
                if stage(n, i, -4) is not None and i == NT - 1:
                    offsets(n + 1)

            slots(pe, slot)
            pe.wait_ge(flag_s, 3)
            pe.matmul(off_ps[:, 0:1], ones[:], flag_f[:, 2:3], start=True, stop=True).then_inc(flag_ps, 1)

            with pe.If(overflowed(pe)):
                def tile(t):
                    wait(pe, lw_turning, t + 1)
                    wait(pe, WhT_kept, t)
                    for k in range(K):
                        last = pe.transpose(turn_ps[:, k * P:k * P + P], lw[:, k * P:k * P + P], ident[:])
                    last.then_inc(lw_turned, 1)
                    wait(pe, diag_ready, t + 1)
                    wait(pe, nrow_kept, t)
                    pe.matmul(nrow_ps[:, 0:P], ones[:], diag, start=True, stop=True).then_inc(nrow_done, 1)

                tile(0)
                with pe.Fori(1, T) as t:
                    tile(t)
                def tile(t):
                    q = t * NCH
                    wait(pe, lw_ready, t + 1)
                    for c in range(NCH):
                        wait(pe, sim_ready, q + c)
                        for k in range(K):
                            last = pe.matmul(s_ps[:], lw[:, k * P:k * P + P], WhT[:, k, c * CH:c * CH + CH],
                                             start=k == 0, stop=k == K - 1)
                        last.then_inc(s_done, 1)
                        wait(pe, p_ready, q + c + 1)
                        wait(pe, pT_ready, q + c)
                        for b in range(B):
                            last = pe.transpose(pT_ps[:, b * P:b * P + P], pr[:, b * P:b * P + P], ident[:])
                        last.then_inc(pT_done, 1)
                        wait(pe, pT_ready, q + c + 1)
                        for b in range(B):
                            last = pe.matmul(pv_ps[:, 0:D + 1], pT[:, b * P:b * P + P], Wh[:, c * B + b, 0:D + 1],
                                             start=c == 0 and b == 0, stop=c == NCH - 1 and b == B - 1)
                        last.then_inc(pv_done, 1)

                tile(0)
                with pe.Fori(1, T) as t:
                    tile(t)

        QA = Q_ACT * WORDS

        @block.scalar
        def _(act):
            act.dma_start(adj_d[:], bass.AP(tensor=adj.tensor, offset=0, ap=[[N + 1, P], [P * (N + 1), T]]), allow_slow_non_contiguous=True).then_inc(diag_loaded, 16)
            act.preload_act_table_set("sqrt_and_others")
            act.wait_ge(w_turned, 1)
            act.activation(WT[:], info_bank[:].rearrange("p (k d) -> p k d", k=K), ACT.Copy).then_inc(w_ready, 1)

            def keep(g):
                for b in range(2):
                    t = 2 * g + b
                    wait(act, wh_done, t + 1)
                    wait(act, wh_kept, t - 1)
                    act.activation(junk_a[:, b, :], out_ps[b][:, 0:D], ACT.Square, accum_out=nsq[:, bass.ds(t, 1)])
                    act.activation(Wh[:, bass.ds(t, 1), 0:D], out_ps[b][:, 0:D], ACT.Copy).then_inc(wh_kept, 1)

            def compare(a, j, lo=0, hi=QA):
                wait(act, adj_loaded[j], (a - j) * 4 + 16)
                wait(act, packed, a - 1)
                part = act.activation(mask[:, j % 2, lo:hi], adjb[:, j, lo:hi], ACT.Sign, bias=neg_half[:, 0:1])
                if hi == QA:
                    part.then_inc(mask_a, 1)

            def norms(q):
                act.wait_ge(wh_kept, q * XT + XT)
                act.activation(Wh[:, q * XT:q * XT + XT, D + 1], nsq[:, q * XT:q * XT + XT], ACT.Sqrt).then_inc(norm_kept, 1)

            keep(0)
            for q in range(LATE // XPAIRS):
                with act.Fori(max(1, q * XPAIRS), q * XPAIRS + XPAIRS) as g:
                    keep(g)
                norms(q)
            act.wait_ge(const_done, 2)
            for p in range(NT):
                for h in range(2):
                    g = LATE + 2 * p + h
                    keep(g)
                    compare(p, p, h * QA // 2, h * QA // 2 + QA // 2)
                    if g % XPAIRS == XPAIRS - 1:
                        norms(g // XPAIRS)
            act.preload_act_table_set("natural_log_exp_and_others")
            act.wait_ge(self_s, 4)
            act.activation(self_t[:], self_t[:], ACT.Exp).then_inc(self_e, 1)

            compare(NT, 0)

            def slot(n, i):
                t4 = stage(n, i, SUM)
                t5 = stage(n, i, NORM)
                b4, b5 = (i - SUM) % 2, (i - NORM) % 2
                if t4 is not None:
                    wait(act, dot_s, 7 * t4 + 7)
                    wait(act, o_ready, t4 - 1)
                    act.activation(we[:, b4, :], sim[:, b4, :], ACT.Exp).then_inc(we_ready, 1)
                if t5 is not None:
                    wait(act, rinv_ready, t5 + 1)
                    wait(act, z_ready, t5 - 1)
                    act.activation(ysb[:, b5, :], out_ps[b5][:, 0:D], ACT.Copy, scale=rinv[:, b5:b5 + 1]).then_inc(y_ready, 1)
                if t4 is not None:
                    wait(act, out_done, t4 - 1)
                    act.activation(dself[:, b4, :], ident[:], ACT.Copy, scale=wself[:, bass.ds(t4, 1)]).then_inc(dself_ready, 1)
                t = stage(n, i, OUT)
                if t is not None:
                    b = (i - OUT) % 2
                    wait(act, shift_ready, t + 1)
                    wait(act, stored[b], 16 * half(n, i, OUT))
                    act.activation(yo[:, b, :], z[:, b, :], ACT.Identity, scale=rstd[:, b:b + 1],
                                   bias=shift[:, b:b + 1]).then_inc(yo_ready, 1)
                a = stage(n, i, -5)
                if a is not None:
                    compare(a, (i + 1) % NT)
                t = stage(n, i, 0)
                if t is not None:
                    wait(act, info_e, t + 1)
                    wait(act, o_ready, t - 3)
                    act.activation(einfo[:, i, :, :], info_ps, ACT.Copy).then_inc(einfo_ready, 1)
                if t5 is not None:
                    wait(act, bn_s, 2 * t5 + 2)
                    act.activation(lnv[:, b5:b5 + 1], mv[:, b5, 1:2], ACT.Ln, bias=ln_eps[:, 0:1]).then_inc(ln_s, 1)
                    wait(act, ln_s, 2 * t5 + 1)
                    act.activation(rstd[:, b5:b5 + 1], lnv[:, b5:b5 + 1], ACT.Exp, scale=-0.5).then_inc(ln_s, 1)

            slots(act, slot)

            with act.If(overflowed(act)):
                def tile(t):
                    wait(act, lw_turned, t)
                    act.activation(lw, Wh[:, bass.ds(t, 1), 0:D].rearrange("p a d -> p (a d)"), ACT.Copy).then_inc(lw_turning, 1)
                    wait(act, lw_turned, t + 1)
                    act.activation(WhT[:, :, bass.ds(t * P, P)], turn_ps[:, 0:D].rearrange("p (k c) -> p k c", k=K),
                                   ACT.Copy).then_inc(WhT_kept, 1)

                tile(0)
                with act.Fori(1, T) as t:
                    tile(t)
                act.wait_ge(WhT_kept, T)
                act.wait_ge(nrow_kept, T)
                act.sem_inc(tile_free, 1)
                def tile(t):
                    q = t * NCH
                    wait(act, tile_free, t + 1)
                    act.activation(lw.rearrange("p (k c) -> p k c", k=K), WhT[:, :, bass.ds(t * P, P)], ACT.Copy).then_inc(lw_ready, 1)
                    for c in range(NCH):
                        wait(act, sim_ready, q + c + 1)
                        wait(act, p_ready, q + c)
                        act.activation(ex, sim_d, ACT.Exp).then_inc(ex_ready, 1)
                        wait(act, pT_done, q + c + 1)
                        wait(act, pv_done, q + c)
                        act.activation(pT, pT_ps[:], ACT.Copy).then_inc(pT_ready, 1)
                    wait(act, fin, 6 * t + 5)
                    act.activation(sm[:, 0:1], mv[:, 0, 1:2], ACT.Ln, bias=ln_eps[:, 0:1]).then_inc(lnv_d, 1)
                    wait(act, lnv_d, t + 1)
                    act.activation(sm[:, 1:2], sm[:, 0:1], ACT.Exp, scale=-0.5).then_inc(rstd_d, 1)
                    wait(act, fin, 6 * t + 6)
                    act.activation(yo[:, 0, :], z[:, 0, :], ACT.Identity, scale=sm[:, 1:2], bias=sm[:, 2:3]).then_inc(out_ready, 1)

                tile(0)
                with act.Fori(1, T) as t:
                    tile(t)

        @block.vector
        def _(dve):
            def compare(a, j):
                wait(dve, adj_loaded[j], (a - j) * 4 + 16)
                wait(dve, packed, a - 1)
                dve.tensor_scalar(mask[:, j % 2, QA:N], adjb[:, j, QA:N], 0.0, 0.5, ALU.is_gt, ALU.subtract).then_inc(mask_v, 1)

            def find(a, j, step):
                keys = pack_ps[j % 2][:, 0:WORDS]
                if step == 0:
                    wait_alone(dve, "dve", packed, a + 1)
                    dve.max(KK[:, j, 0:8], keys).then_inc(find_s, 1)
                if step == 1:
                    wait_alone(dve, "dve", find_s, 3 * a + 1)
                    dve.match_replace(out=keys_left[:], in_to_replace=KK[:, j, 0:8], in_values=keys, imm_value=0.0).then_inc(find_s, 1)
                if step == 2:
                    wait_alone(dve, "dve", find_s, 3 * a + 2)
                    dve.max(KK[:, j, 8:16], keys_left[:]).then_inc(find_s, 1)

            def hand(t, b):
                dve.tensor_copy(xs[:, b, :], X[:, bass.ds(t, 1), :].rearrange("p a d -> p (a d)")).then_inc(xs_ready, 1)

            def turned(g, more=True):
                for b in range(2):
                    t = 2 * g + b
                    wait(dve, x_turned, t + 1)
                    if more:
                        hand(t + 2, b)
                    wait(dve, wh_done, t - 1)
                    dve.tensor_copy(xT[:, b, :], a_ps[b][:, 0:D]).then_inc(xT_ready, 1)

            dve.wait_ge(x_loaded[0], 16)
            for b in range(2):
                hand(b, b)
            turned(0)
            for q in range(LATE // XPAIRS):
                with dve.Fori(max(1, q * XPAIRS), q * XPAIRS + XPAIRS - 1) as g:
                    turned(g)
                dve.wait_ge(x_loaded[q + 1], 16)
                turned(q * XPAIRS + XPAIRS - 1)
                if q == 0:
                    for w_q in range(BITS):
                        weight = float(2 ** (w_q + 7)) if w_q < Q_ACT else float(2 ** (w_q + 8))
                        last = dve.tensor_scalar(bit_w[:, w_q, :], ident[:], weight, None, ALU.mult)
                    last.then_inc(bits_done, 1)
                    dve.memset(info[:, :, 0:I_ROW], 0.0)
                    dve.memset(ov_k[:], 0.0)
                    dve.memset(ov_e[:], 0.0)
            for p in range(NT):
                for g in range(LATE + 2 * p, LATE + 2 * p + 2):
                    if g < T // 2 - 1 and (g + 1) % XPAIRS == 0:
                        dve.wait_ge(x_loaded[(g + 1) // XPAIRS], 16)
                    turned(g, g < T // 2 - 1)
                compare(p, p)
                if p > 0:
                    for k in range(3):
                        find(p - 1, p - 1, k)
            dve.wait_ge(norm_kept, XC)
            norm = Wh[:, :, D + 1]
            dve.tensor_tensor(self_t[:], norm, norm, ALU.mult).then_inc(self_s, 1)
            dve.wait_ge(self_s, 1)
            dve.tensor_scalar(self_t[:], self_t[:], SIM_EPS, None, ALU.add).then_inc(self_s, 1)
            dve.wait_ge(self_s, 2)
            dve.reciprocal(self_t[:], self_t[:]).then_inc(self_s, 1)
            dve.wait_ge(self_s, 3)
            dve.tensor_tensor(self_t[:], nsq[:], self_t[:], ALU.mult).then_inc(self_s, 1)
            dve.wait_ge(diag_loaded, 16)
            dve.wait_ge(self_e, 1)
            dve.scalar_tensor_tensor(out=wself[:], in0=adj_d[:], scalar=0.0, in1=self_t[:], op0=ALU.is_le,
                                     op1=ALU.mult).then_inc(self_s, 1)
            dve.wait_ge(self_s, 5)
            dve.tensor_scalar(wself[:], wself[:], TINY, None, ALU.max).then_inc(self_s, 1)

            def find_batch(nb):
                s0 = B_OPS * nb
                k = [0]

                def step(ins):
                    k[0] += 1
                    ins.then_inc(batch_s, 1)

                def settle(alone=False):
                    (wait_alone(dve, "dve", batch_s, s0 + k[0]) if alone else wait(dve, batch_s, s0 + k[0]))

                def level(k1, rest):
                    key = KK[:, :, k1 * K1:k1 * K1 + K1]
                    step(dve.tensor_scalar(key_p[:], key.bitcast(I32), EXP_BITS, None, ALU.bitwise_and))
                    settle()
                    step(dve.tensor_tensor(rest, key, key_p[:].bitcast(F32), ALU.subtract))

                wait(dve, find_s, 3 * (4 * nb + 4))
                level(0, KK[:, :, K1:2 * K1])
                settle()
                level(1, KK[:, :, 2 * K1:3 * K1])
                settle(True)
                for j in range(NT):
                    last = dve.max(KK[:, j, LIST + 8:LIST + 16], KK[:, j, 0:KEYS])
                step(last)
                level(2, key_r[:])
                settle(True)
                for j in range(NT):
                    last = dve.match_replace(out=V_left[:, j, :], in_to_replace=KK[:, j, LIST + 8:LIST + 16],
                                             in_values=KK[:, j, 0:KEYS], imm_value=0.0)
                step(last)
                step(dve.tensor_reduce(KK[:, :, LEFT], key_r[:], AX.X, ALU.max))
                wait_alone(dve, "dve", batch_s, s0 + k[0] - 1)
                for j in range(NT):
                    last = dve.max(KK[:, j, LIST:LIST + 8], V_left[:, j, :])
                step(last)
                settle()
                keys = KK[:, :, LIST:LIST + SLOTS]
                step(dve.tensor_scalar(valid[:], keys, LO, None, ALU.is_ge))
                step(dve.tensor_scalar(key_e[:], keys.bitcast(I32), 23, None, ALU.logical_shift_right))
                wait(dve, batch_s, s0 + k[0] - 1)
                if not isinstance(nb, int) or nb > 0:
                    wait(dve, off_done, nb)
                dve.tensor_reduce(cnt[:], valid[:], AX.X, ALU.add).then_inc(cnt_ready, 1)
                step(dve.tensor_copy(key_i[:], keys))
                step(dve.tensor_tensor(ov_k[:], ov_k[:], KK[:, :, K1 - 1:LIST + 8:OV_STEP], ALU.max))
                wait(dve, batch_s, s0 + k[0] - 1)
                step(dve.tensor_scalar(key_i[:], key_i[:], 255, None, ALU.bitwise_and))
                wait(dve, info_e, 4 * nb)
                step(dve.tensor_copy(info[:, :, I_NORM], Wh[:, bass.ds(4 * nb, 4), D + 1]))
                wait(dve, batch_s, s0 + k[0] - 1)
                step(dve.scalar_tensor_tensor(out=info[:, :, 0:SLOTS], in0=key_e[:], scalar=256.0, in1=key_i[:],
                                              op0=ALU.mult, op1=ALU.subtract))
                wait(dve, off_done, nb + 1)
                step(dve.tensor_copy(info[:, :, I_OFF], off_ps))
                wait(dve, cnt_ready, nb + 1)
                step(dve.tensor_tensor(info[:, :, I_END], off_ps, cnt[:], ALU.add))
                settle()
                dve.tensor_tensor(ov_e[:], ov_e[:], info[:, :, I_END], ALU.max).then_inc(info_ready, 1)
                batch_count.append(k[0])

            batch_count = []
            B_OPS = 3 * 2 + 3 + 1 + 9
            compare(NT, 0)
            for k in range(3):
                find(NT - 1, NT - 1, k)
            find_batch(0)
            assert batch_count[0] == B_OPS, batch_count

            def slot(n, i):
                t0, t1, t3, t4, t5, t6 = [stage(n, i, d) for d in (0, GATHER, DOT, SUM, NORM, OUT)]
                ip = einfo[:, (i - GATHER) % 4, :, :]
                b4, g4 = (i - SUM) % 2, (i - SUM) % 4
                b5 = (i - NORM) % 2

                def weigh(c):
                    return dve.tensor_scalar(O[:, b4, c, :], row1_no[:], einfo[:, g4, c, I_ROW:I_ROW + 1], we[:, b4, c:c + 1],
                                             ALU.is_equal, ALU.mult)

                if t5 is not None:
                    wait(dve, out_done, t5 + 1)
                    wait(dve, y_ready, t5 - 1)
                    dve.reciprocal(rinv[:, b5:b5 + 1], out_ps[b5][:, D:D + 1]).then_inc(rinv_ready, 1)
                if t1 is not None:
                    wait(dve, einfo_ready, t1 + 1)
                    wait(dve, j_s, 5 * t1)
                    dve.tensor_tensor(slot_e[:], edge_of[:], ip[:, :, I_OFF], ALU.subtract).then_inc(j_s, 1)
                if t6 is not None:
                    b = (i - OUT) % 2
                    wait(dve, ln_s, 2 * t6 + 2)
                    wait(dve, yo_ready, t6 - 1)
                    dve.scalar_tensor_tensor(out=shift[:, b:b + 1], in0=mv[:, b, 0:1], scalar=-1.0, in1=rstd[:, b:b + 1],
                                             op0=ALU.mult, op1=ALU.mult).then_inc(shift_ready, 1)
                if t1 is not None:
                    wait(dve, j_s, 5 * t1 + 1)
                    dve.tensor_tensor(hit[:], slot_no[:], slot_e[:].rearrange("p (c o) -> p c o", o=1).to_broadcast([P, EC, SLOTS]),
                                      ALU.is_equal).then_inc(j_s, 1)
                if t4 is not None:
                    wait(dve, we_ready, t4 + 1)
                    wait(dve, out_done, t4 - 1)
                    weigh(0)
                if t1 is not None:
                    wait(dve, j_s, 5 * t1 + 2)
                    dve.tensor_tensor(hitj[:], hit[:], ip[:, :, 0:SLOTS], ALU.mult).then_inc(j_s, 1)
                if t4 is not None:
                    weigh(1)
                if t1 is not None:
                    wait(dve, j_s, 5 * t1 + 3)
                    dve.tensor_reduce(jf[:], hitj[:], AX.X, ALU.add).then_inc(j_s, 1)
                if t4 is not None:
                    weigh(2).then_inc(o_ready, 1)
                if t1 is not None:
                    b = (i - GATHER) % 4
                    wait(dve, j_s, 5 * t1 + 4)
                    wait(dve, gathered[b], 48 * (n + (i - GATHER - b) // 4))
                    dve.tensor_scalar(J[:, b, :], jf[:], float(-J_SHIFT), None, ALU.add).then_inc(j_s, 1)
                if t0 is not None:
                    wait(dve, info_ready, n + 1)
                    wait(dve, batch_s, B_OPS * (n + 1))
                    wait(dve, r_s, 2 * t0)
                    dve.tensor_scalar(ge[:], edge_no[:], info[:, i, I_OFF:I_OFF + 1], None, ALU.is_ge).then_inc(r_s, 1)
                if t0 is not None:
                    wait(dve, r_s, 2 * t0 + 1)
                    wait(dve, a_done, t0 - 3)
                    dve.scalar_tensor_tensor(out=R[:, i, :], in0=edge_no[:], scalar=info[:, i, I_END:I_END + 1],
                                             in1=ge[:], op0=ALU.is_lt, op1=ALU.mult).then_inc(r_s, 1)
                a = stage(n, i, -5)
                if a is not None:
                    compare(a, (i + 1) % NT)
                a = stage(n, i, -4)
                if a is not None:
                    find(a, i, 0)
                if t3 is not None:
                    b3 = (i - DOT) % 2
                    g = (i - DOT) % 4
                    wait(dve, a_done, t3 + 1)
                    wait(dve, gathered[g], 48 * (n + (i - DOT - g) // 4 + 1))
                    wait(dve, einfo_ready, t3 + 1)

                    def product(c):
                        dve.tensor_tensor_reduce(junk[:, c, :], G[:, g, c, 0:D], A_chunk(c), 1.0, 0.0, ALU.mult, ALU.add,
                                                 dot[:, c:c + 1]).then_inc(dot_s, 1)

                    wait(dve, dot_s, 7 * t3)
                    dve.tensor_tensor(nn[:], G[:, g, :, D + 1], einfo[:, g, :, I_NORM], ALU.mult).then_inc(dot_s, 1)
                    product(0)
                if a is not None:
                    find(a, i, 1)
                if t3 is not None:
                    wait(dve, dot_s, 7 * t3 + 1)
                    dve.tensor_scalar(nn[:], nn[:], SIM_EPS, None, ALU.add).then_inc(dot_s, 1)
                    product(1)
                if t5 is not None:
                    wait(dve, z_ready, t5 + 1)
                    wait(dve, bn_s, 2 * t5)
                    dve.bn_stats(st[:], z[:, b5, :]).then_inc(bn_s, 1)
                if a is not None:
                    find(a, i, 2)
                if t3 is not None:
                    wait(dve, dot_s, 7 * t3 + 3)
                    dve.reciprocal(nn[:], nn[:]).then_inc(dot_s, 1)
                    product(2)
                if t5 is not None:
                    wait_alone(dve, "dve", bn_s, 2 * t5 + 1)
                    wait_alone(dve, "dve", yo_ready, t5 - 1)
                    dve.bn_aggr(mv[:, b5, :], st[:]).then_inc(bn_s, 1)
                if t3 is not None:
                    wait(dve, dot_s, 7 * t3 + 6)
                    wait(dve, we_ready, t3 - 1)
                    dve.tensor_tensor(sim[:, b3, :], dot[:], nn[:], ALU.mult).then_inc(dot_s, 1)
                if a is not None and i == NT - 1:
                    find_batch(n + 1)

            slots(dve, slot)
            dve.tensor_reduce(flag_f[:, 0:1], ov_k[:], AX.XY, ALU.max)
            dve.tensor_reduce(flag_f[:, 1:2], ov_e[:], AX.X, ALU.max).then_inc(flag_s, 1)
            dve.wait_ge(flag_s, 1)
            dve.tensor_scalar(flag_f[:, 0:1], flag_f[:, 0:1], LO, None, ALU.is_ge).then_inc(flag_s, 1)
            dve.wait_ge(flag_s, 2)
            dve.scalar_tensor_tensor(out=flag_f[:, 2:3], in0=flag_f[:, 1:2], scalar=float(EDGES), in1=flag_f[:, 0:1],
                                     op0=ALU.is_gt, op1=ALU.add).then_inc(flag_s, 1)
            dve.wait_ge(flag_ps, 1)
            if force_dense:
                dve.tensor_scalar(flag[:], off_ps[:, 0:1], 0.0, 1.0, ALU.is_gt, ALU.max).then_inc(flag_ready, 1)
            else:
                dve.tensor_scalar(flag[:], off_ps[:, 0:1], 0.0, None, ALU.is_gt).then_inc(flag_ready, 1)

            with dve.If(overflowed(dve)):
                def tile(t):
                    wait(dve, nrow_done, t)
                    dve.tensor_scalar(diag, ident[:], Wh[:, bass.ds(t, 1), D + 1:D + 2].rearrange("p a b -> p (a b)"),
                                      None, ALU.mult).then_inc(diag_ready, 1)
                    wait(dve, nrow_done, t + 1)
                    dve.tensor_copy(norm_row[:, bass.ds(t * P, P)], nrow_ps[:, 0:P]).then_inc(nrow_kept, 1)

                tile(0)
                with dve.Fori(1, T) as t:
                    tile(t)
                dve.wait_ge(nrow_kept, T)
                dve.wait_ge(WhT_kept, T)
                def tile(t):
                    q = t * NCH
                    ni = Wh[:, bass.ds(t, 1), D + 1:D + 2].rearrange("p a b -> p (a b)")
                    own = adj_row[:, bass.ds(t * P, P)]
                    wait(dve, tile_free, t + 1)
                    wait(dve, row_loaded, 16 * t + 16)
                    dve.tensor_tensor(own, own, ident[:], ALU.max).then_inc(diag_set, 1)
                    wait(dve, diag_set, t + 1)
                    for c in range(NCH):
                        cs = slice(c * CH, c * CH + CH)
                        wait(dve, sim_ready, q + c)
                        dve.tensor_scalar(den, norm_row[:, cs], ni, SIM_EPS, ALU.mult, ALU.add).then_inc(den_ready, 1)
                        wait(dve, den_ready, q + c + 1)
                        dve.reciprocal(rec, den).then_inc(rec_ready, 1)
                        wait(dve, rec_ready, q + c + 1)
                        wait(dve, s_done, q + c + 1)
                        wait(dve, ex_ready, q + c)
                        dve.tensor_tensor(sim_d, s_ps[:], rec, ALU.mult).then_inc(sim_ready, 1)
                        wait(dve, ex_ready, q + c + 1)
                        wait(dve, pT_done, q + c)
                        dve.scalar_tensor_tensor(out=pr, in0=adj_row[:, cs], scalar=0.0, in1=ex, op0=ALU.is_gt,
                                                 op1=ALU.mult).then_inc(p_ready, 1)
                    e = 6 * t
                    wait(dve, pv_done, q + NCH)
                    dve.reciprocal(sm[:, 3:4], pv_ps[:, D:D + 1]).then_inc(fin, 1)
                    wait(dve, fin, e + 1)
                    dve.tensor_scalar(ysb[:, 0, :], pv_ps[:, 0:D], sm[:, 3:4], None, ALU.mult).then_inc(fin, 1)
                    wait(dve, fin, e + 2)
                    dve.tensor_tensor(z[:, 0, :], ysb[:, 0, :], X[:, bass.ds(t, 1), :].rearrange("p a b -> p (a b)"),
                                      ALU.add).then_inc(fin, 1)
                    wait(dve, fin, e + 3)
                    dve.bn_stats(st[:], z[:, 0, :]).then_inc(fin, 1)
                    wait_alone(dve, "dve", fin, e + 4)
                    dve.bn_aggr(mv[:, 0, :], st[:]).then_inc(fin, 1)
                    wait(dve, fin, e + 5)
                    wait(dve, rstd_d, t + 1)
                    dve.scalar_tensor_tensor(out=sm[:, 2:3], in0=mv[:, 0, 0:1], scalar=-1.0, in1=sm[:, 1:2],
                                             op0=ALU.mult, op1=ALU.mult).then_inc(fin, 1)

                tile(0)
                with dve.Fori(1, T) as t:
                    tile(t)


_INS = ["x", "adj", "L0_gnn_W"]


def kernel(**inputs):
    import numpy as _np
    import concourse.bacc as _bacc
    from concourse import mybir as _mybir
    from concourse.bass_utils import run_bass_kernel_spmd as _run

    nc = _bacc.Bacc("TRN2", target_bir_lowering=False, num_devices=1)
    arrays, args = {}, []
    for name in _INS:
        a = _np.ascontiguousarray(inputs[name])
        arrays[f"in_{name}"] = a
        args.append(nc.dram_tensor(f"in_{name}", a.shape, _mybir.dt.from_np(a.dtype), kind="ExternalInput").ap())
    o = nc.dram_tensor("out_0", inputs["x"].shape, _mybir.dt.float32, kind="ExternalOutput").ap()
    gnn_layer(nc, *args, o)
    r = _run(nc, [arrays], core_ids=[0])
    return r.results[0]["out_0"]
```

```python
from contextlib import ExitStack

import concourse.bass as bass
from concourse import mybir

ALU = mybir.AluOpType
ACT = mybir.ActivationFunctionType
AX = mybir.AxisListType
F32 = mybir.dt.float32
F16 = mybir.dt.float16
BF16 = mybir.dt.bfloat16
I32 = mybir.dt.int32
U32 = mybir.dt.uint32
P = 128
SIM_EPS = 1e-8
LN_EPS = 1e-5
TINY = 1e-30

WORDS = 256
BITS = 16
LO = 256.0
EXP_BITS = 0x7F800000
J_SHIFT = 256 * (127 + 8) - 255
K1 = 16
SLOTS = 16
KEYS = 3 * K1
LEFT = KEYS
LIST = 2 * LEFT - K1 - 6
OV_STEP = LEFT - K1 + 1
EC = 3
EDGES = EC * P
INFO = 20
I_OFF, I_NORM, I_ROW, I_END = 16, 17, 18, 19
NT = 4
Q_ACT = 14
LOAD, COMPARE, FIND = -8, -5, -4
GATHER, DOT, SUM, NORM, OUT = 1, 3, 4, 5, 6


def wait(eng, s, v):
    if not isinstance(v, int) or v > 0:
        eng.wait_ge(s, v)


def gnn_layer(nc, x, adj, w, out):
    N, D = x.shape
    T = N // P
    K = D // P
    NB = T // NT
    XC = 4
    XPAIRS = T // XC // 2
    LATE = T // 2 - 2 * NT
    XT = T // XC
    ROW = D + 2
    x_t = x.rearrange("(t p) d -> p t d", p=P)
    adj_t = adj.rearrange("(t p) j -> p t j", p=P)
    out_t = out.rearrange("(t p) d -> p t d", p=P)
    w_h = w.rearrange("(h p) d -> p h d", p=P)
    wh_rows = nc.dram_tensor("wh_rows", (N, ROW), F32, kind="Internal").ap()
    wh_rows_t = wh_rows.rearrange("(t p) d -> p t d", p=P)

    with ExitStack() as ctx:
        def sb(name, shape, dt=F32):
            return ctx.enter_context(nc.sbuf_tensor(name, shape, dt))

        def ps(name, shape, dt=F32):
            return ctx.enter_context(nc.psum_tensor(name, shape, dt))

        def sem(name):
            return ctx.enter_context(nc.semaphore(name))

        ident = sb("ident", [P, P])
        ones = sb("ones", [P, P])
        tri = sb("tri", [P, P])
        bit_w = sb("bit_w", [P, BITS, P], BF16)
        bias_rows = sb("bias_rows", [P, WORDS], BF16)
        ones_b = sb("ones_b", [P, P], BF16)
        edge_no = sb("edge_no", [P, EDGES], F16)
        edge_of = sb("edge_of", [P, EC])
        slot_no = sb("slot_no", [P, EC, SLOTS])
        row1_no = sb("row1_no", [P, P])
        iota_i = sb("iota_i", [P, EDGES], I32)
        ln_eps = sb("ln_eps", [P, 1])
        neg_half = sb("neg_half", [P, 1])
        X = sb("X", [P, T, D])
        Wh = sb("Wh", [P, T, ROW])
        nsq = sb("nsq", [P, T])
        adj_d = sb("adj_d", [P, T], I32)
        wself = sb("wself", [P, T])
        self_t = sb("self_t", [P, T])
        xs = sb("xs", [P, 2, D])
        wsb = sb("wsb", [P, K, D])
        WT = sb("WT", [P, K, D])
        xT = sb("xT", [P, 2, D])
        junk = sb("junk", [P, EC, D])
        junk_a = sb("junk_a", [P, 2, D])
        adjb = sb("adjb", [P, NT, N], I32)
        mask = sb("mask", [P, 2, N], BF16)
        keys_left = sb("keys_left", [P, WORDS])
        KK = sb("KK", [P, NT, LIST + SLOTS])
        key_i = sb("key_i", [P, NT, K1], I32)
        key_e = sb("key_e", [P, NT, K1], I32)
        key_p = sb("key_p", [P, NT, K1], I32)
        key_r = sb("key_r", [P, NT, K1])
        V_left = sb("V_left", [P, NT, KEYS])
        valid = sb("valid", [P, NT, SLOTS])
        cnt = sb("cnt", [P, NT])
        info = sb("info", [P, NT, INFO])
        ov_k = sb("ov_k", [P, NT, 3])
        ov_e = sb("ov_e", [P, NT])
        ge = sb("ge", [P, EDGES], F16)
        R = sb("R", [P, 4, EDGES])
        slot_e = sb("slot_e", [P, EC])
        hit = sb("hit", [P, EC, SLOTS])
        hitj = sb("hitj", [P, EC, SLOTS])
        jf = sb("jf", [P, EC])
        J = sb("J", [P, 4, EC], I32)
        einfo = sb("einfo", [P, 4, EC, INFO])
        G = sb("G", [P, 4, EC, ROW])
        dot = sb("dot", [P, EC])
        nn = sb("nn", [P, EC])
        sim = sb("sim", [P, 2, EC])
        we = sb("we", [P, 2, EC])
        O = sb("O", [P, 2, EC, P])
        dself = sb("dself", [P, 2, P])
        rinv = sb("rinv", [P, 2])
        ysb = sb("ysb", [P, 2, D])
        z = sb("z", [P, 2, D])
        st = sb("st", [P, 6])
        mv = sb("mv", [P, 2, 2])
        lnv = sb("lnv", [P, 2])
        rstd = sb("rstd", [P, 2])
        shift = sb("shift", [P, 2])
        yo = sb("yo", [P, 2, D])
        flag_f = sb("flag_f", [P, 4])
        flag = sb("flag", [P, 1], I32)

        pack_ps = [ps(f"pack_ps{i}", [P, 512]) for i in range(2)]
        a_ps = [ps(f"a_ps{i}", [P, 512]) for i in range(2)]
        out_ps = [ps(f"out_ps{i}", [P, 512]) for i in range(2)]
        info_bank = ps("info_bank", [P, 512])
        off_bank = ps("off_bank", [P, 512])
        off_ps = off_bank[:, 0:NT]
        info_ps = info_bank[:, 0:EC * INFO].rearrange("p (c f) -> p c f", c=EC)

        def A_chunk(c):
            return a_ps[c // 2][:, (c % 2) * D:(c % 2) * D + D]

        w_loaded = sem("w_loaded")
        diag_loaded = sem("diag_loaded")
        pool_c = sem("pool_c")
        const_done = sem("const_done")
        bits_done = sem("bits_done")
        x_loaded = [sem(f"x_loaded{q}") for q in range(XC)]
        xs_ready = sem("xs_ready")
        norm_kept = sem("norm_kept")
        x_turned = sem("x_turned")
        xT_ready = sem("xT_ready")
        wh_done = sem("wh_done")
        wh_kept = sem("wh_kept")
        rows_stored = sem("rows_stored")
        w_turned = sem("w_turned")
        w_ready = sem("w_ready")
        self_s = sem("self_s")
        self_e = sem("self_e")
        adj_loaded = [sem(f"adj_loaded{b}") for b in range(NT)]
        mask_a = sem("mask_a")
        mask_v = sem("mask_v")
        packed = sem("packed")
        find_s = sem("find_s")
        batch_s = sem("batch_s")
        cnt_ready = sem("cnt_ready")
        off_done = sem("off_done")
        info_ready = sem("info_ready")
        r_s = sem("r_s")
        info_e = sem("info_e")
        a_done = sem("a_done")
        j_s = sem("j_s")
        einfo_ready = sem("einfo_ready")
        gathered = [sem(f"gathered{b}") for b in range(4)]
        dot_s = sem("dot_s")
        we_ready = sem("we_ready")
        o_ready = sem("o_ready")
        dself_ready = sem("dself_ready")
        out_done = sem("out_done")
        rinv_ready = sem("rinv_ready")
        y_ready = sem("y_ready")
        z_ready = sem("z_ready")
        bn_s = sem("bn_s")
        ln_s = sem("ln_s")
        shift_ready = sem("shift_ready")
        yo_ready = sem("yo_ready")
        stored = [sem(f"stored{b}") for b in range(2)]
        flag_s = sem("flag_s")
        flag_ps = sem("flag_ps")
        flag_ready = sem("flag_ready")
        passed = {e: sem(f"passed_{e}") for e in ("dve", "pool", "act")}

        CH = 512
        NCH = N // CH
        B = CH // P
        adj_row = adjb[:, 0, :]
        norm_row = adjb[:, 1, :].bitcast(F32)
        WhT = adjb[:, 2:2 + K, :].bitcast(F32)
        free = mask[:].rearrange("p b n -> p (b n)").bitcast(F32)
        den, rec, sim_d, ex, pr, pT = [free[:, i * CH:i * CH + CH] for i in range(6)]
        lw = free[:, 6 * CH:6 * CH + D]
        diag = free[:, 6 * CH + D:6 * CH + D + P]
        sm = sb("sm", [P, 4])
        turn_ps, nrow_ps = pack_ps
        s_ps, pT_ps = a_ps
        pv_ps = out_ps[0]
        lw_turning = sem("lw_turning")
        lw_turned = sem("lw_turned")
        WhT_kept = sem("WhT_kept")
        diag_ready = sem("diag_ready")
        nrow_done = sem("nrow_done")
        nrow_kept = sem("nrow_kept")
        row_loaded = sem("row_loaded")
        tile_stored = sem("tile_stored")
        tile_free = sem("tile_free")
        lw_ready = sem("lw_ready")
        s_done = sem("s_done")
        den_ready = sem("den_ready")
        rec_ready = sem("rec_ready")
        sim_ready = sem("sim_ready")
        ex_ready = sem("ex_ready")
        diag_set = sem("diag_set")
        p_ready = sem("p_ready")
        pT_done = sem("pT_done")
        pT_ready = sem("pT_ready")
        pv_done = sem("pv_done")
        fin = sem("fin")
        lnv_d = sem("lnv_d")
        rstd_d = sem("rstd_d")
        out_ready = sem("out_ready")

        def overflowed(eng):
            eng.wait_ge(flag_ready, 1)
            return eng.value_load(flag[0:1, 0:1], min_val=0, max_val=1) > 0

        def wait_alone(eng, e, s, v):
            if not isinstance(v, int) or v > 0:
                eng.wait_ge(s, v)
                if not isinstance(v, int):
                    eng.sem_inc(passed[e], 1)

        block = ctx.enter_context(nc.Block())

        def slots(eng, slot):
            for n in range(2):
                for i in range(NT):
                    slot(n, i)
            with eng.Fori(2, NB - 2) as n:
                for i in range(NT):
                    slot(n, i)
            for n in range(NB - 2, NB + 2):
                for i in range(NT):
                    slot(n, i)

        def stage(n, i, d):
            t = 4 * n + (i - d)
            if isinstance(n, int) and not 0 <= t < T:
                return None
            return t

        def half(n, i, d):
            return 2 * n + (i - d) // 2

        @block.sync
        def _(sp):
            sp.dma_start(wsb[:], w_h).then_inc(w_loaded, 16)
            for q in range(XC):
                sp.dma_start(X[:, q * XT:q * XT + XT, :], x_t[:, q * XT:q * XT + XT, :]).then_inc(x_loaded[q], 16)
            for i in range(NT):
                sp.dma_start(adjb[:, i, :], adj_t[:, i, :]).then_inc(adj_loaded[i], 16)

            def slot(n, i):
                a = stage(n, i, LOAD)
                if a is not None:
                    wait(sp, mask_a, a - NT + 1)
                    wait(sp, mask_v, a - NT + 1)
                    sp.dma_start(adjb[:, i, :], adj_t[:, bass.ds(a, 1), :]).then_inc(adj_loaded[i], 16)
                t = stage(n, i, OUT)
                if t is not None:
                    b = (i - OUT) % 2
                    wait(sp, yo_ready, t + 1)
                    sp.dma_start(out_t[:, bass.ds(t, 1), :], yo[:, b, :]).then_inc(stored[b], 16)

            for i in range(NT):
                wait(sp, mask_a, i + 1)
                wait(sp, mask_v, i + 1)
                sp.dma_start(adjb[:, i, :], adj_t[:, NT + i, :]).then_inc(adj_loaded[i], 16)
            slots(sp, slot)
            for b in range(2):
                sp.wait_ge(stored[b], 16 * (T // 2))

            with sp.If(overflowed(sp)):
                def tile(t):
                    wait(sp, tile_free, t + 1)
                    sp.dma_start(adj_row, adj_t[:, bass.ds(t, 1), :]).then_inc(row_loaded, 16)
                    wait(sp, out_ready, t + 1)
                    sp.dma_start(out_t[:, bass.ds(t, 1), :], yo[:, 0, :]).then_inc(tile_stored, 16)
                    wait(sp, tile_stored, 16 * t + 16)
                    sp.sem_inc(tile_free, 1)

                tile(0)
                with sp.Fori(1, T) as t:
                    tile(t)

        @block.gpsimd
        def _(pool):
            pool.memset(ident[:], 0.0).then_inc(pool_c, 1)
            pool.wait_ge(pool_c, 1)
            pool.affine_select(out=ident[:], in_=ident[:], compare_op=ALU.not_equal, fill=1.0, base=0,
                               pattern=[[-1, P]], channel_multiplier=1).then_inc(const_done, 1)
            pool.memset(ones[:], 1.0)
            pool.memset(ones_b[:], 1.0)
            pool.memset(ln_eps[:], LN_EPS)
            pool.memset(neg_half[:], -0.5)
            pool.memset(Wh[:, :, D:D + 1], 1.0)
            pool.memset(tri[:], 1.0)
            pool.memset(bias_rows[:], 0.0).then_inc(pool_c, 1)
            pool.wait_ge(pool_c, 2)
            pool.affine_select(out=tri[:], in_=tri[:], compare_op=ALU.is_gt, fill=0.0, base=0,
                               pattern=[[1, P]], channel_multiplier=-1)
            pool.iota(iota_i[:, 0:WORDS], pattern=[[-1, WORDS]], base=WORDS - 1, channel_multiplier=0).then_inc(pool_c, 1)
            pool.wait_ge(pool_c, 3)
            pool.tensor_copy(bias_rows[0:1, :], iota_i[0:1, 0:WORDS]).then_inc(pool_c, 1)
            pool.wait_ge(pool_c, 4)
            pool.affine_select(out=bias_rows[:], in_=bias_rows[:], compare_op=ALU.not_equal, fill=float(2 ** 23),
                               base=-1, pattern=[[0, WORDS]], channel_multiplier=1).then_inc(pool_c, 1)
            pool.wait_ge(pool_c, 5)
            pool.affine_select(out=bias_rows[:], in_=bias_rows[:], compare_op=ALU.not_equal, fill=-128.0,
                               base=-2, pattern=[[0, WORDS]], channel_multiplier=1)
            pool.iota(iota_i[:], pattern=[[1, EDGES]], base=0, channel_multiplier=0).then_inc(pool_c, 1)
            pool.wait_ge(pool_c, 6)
            pool.tensor_copy(edge_no[:], iota_i[:])
            for c in range(EC):
                pool.tensor_copy(slot_no[:, c, 0:8], iota_i[:, 8:SLOTS])
                pool.tensor_copy(slot_no[:, c, 8:SLOTS], iota_i[:, 0:8])
            pool.tensor_copy(row1_no[:], iota_i[:, 1:P + 1]).then_inc(pool_c, 1)
            pool.wait_ge(pool_c, 7)
            pool.iota(iota_i[:, 0:EC], pattern=[[P, EC]], base=0, channel_multiplier=1).then_inc(pool_c, 1)
            pool.wait_ge(pool_c, 8)
            pool.tensor_copy(edge_of[:], iota_i[:, 0:EC]).then_inc(pool_c, 1)
            pool.wait_ge(pool_c, 9)
            pool.iota(iota_i[:, 0:1], pattern=[[0, 1]], base=1, channel_multiplier=1).then_inc(pool_c, 1)
            pool.wait_ge(pool_c, 10)
            for j in range(NT):
                last = pool.tensor_copy(info[:, j, I_ROW:I_ROW + 1], iota_i[:, 0:1])
            last.then_inc(const_done, 1)
            pool.memset(G[:], 0.0).then_inc(pool_c, 1)
            for q in range(XC):
                pool.wait_ge(norm_kept, q + 1)
                pool.dma_start(wh_rows_t[:, q * XT:q * XT + XT, :], Wh[:, q * XT:q * XT + XT, :]).then_inc(rows_stored, 16)

            pool.wait_ge(pool_c, 11)
            pool.wait_ge(rows_stored, 16 * XC)

            def slot(n, i):
                t = stage(n, i, NORM)
                if t is not None:
                    b = (i - NORM) % 2
                    wait_alone(pool, "pool", y_ready, t + 1)
                    wait_alone(pool, "pool", yo_ready, t - 1)
                    pool.tensor_tensor(z[:, b, :], ysb[:, b, :],
                                       X[:, bass.ds(t, 1), :].rearrange("p a d -> p (a d)"), ALU.add).then_inc(z_ready, 1)
                t = stage(n, i, GATHER)
                if t is not None:
                    b = (i - GATHER) % 4
                    wait_alone(pool, "pool", j_s, 5 * t + 5)
                    wait_alone(pool, "pool", out_done, t - 3)
                    for c in range(EC):
                        pool.indirect_dma_start(
                            out=G[:, b, c, :], out_offset=None, in_=wh_rows,
                            in_offset=bass.IndirectOffsetOnAxis(ap=J[:, b, c:c + 1].bitcast(U32), axis=0),
                            bounds_check=N - 1, oob_is_err=False).then_inc(gathered[b], 16)

            slots(pool, slot)

        @block.tensor
        def _(pe):
            pe.wait_ge(const_done, 1)
            pe.wait_ge(w_loaded, 16)
            for h in range(K):
                for k in range(K):
                    last = pe.transpose(info_bank[:, k * D + h * P:k * D + h * P + P], wsb[:, h, k * P:k * P + P], ident[:])
            last.then_inc(w_turned, 1)
            pe.wait_ge(w_ready, 1)

            def turn(g, b):
                wait(pe, xs_ready, 2 * g + b + 1)
                wait(pe, xT_ready, 2 * g + b - 1)
                for k in range(K):
                    last = pe.transpose(a_ps[b][:, k * P:k * P + P], xs[:, b, k * P:k * P + P], ident[:])
                last.then_inc(x_turned, 1)

            def project(g, b):
                wait(pe, xT_ready, 2 * g + b + 1)
                wait(pe, wh_kept, 2 * g + b - 1)
                for k in range(K):
                    last = pe.matmul(out_ps[b][:, 0:D], xT[:, b, k * P:k * P + P], WT[:, k, :],
                                     start=k == 0, stop=k == K - 1)
                last.then_inc(wh_done, 1)

            def turn_and_project(g):
                for b in range(2):
                    turn(g, b)
                    project(g - 1, b)

            def pack(a, j):
                b = j % 2
                wait(pe, mask_a, a + 1)
                wait(pe, mask_v, a + 1)
                wait(pe, find_s, 3 * (a - 1))
                for q in range(BITS):
                    pe.matmul(pack_ps[b][:, 0:WORDS], bit_w[:, q, :], mask[:, b, q * WORDS:q * WORDS + WORDS],
                              start=q == 0, stop=False)
                pe.matmul(pack_ps[b][:, 0:WORDS], ones_b[:], bias_rows[:], start=False, stop=True).then_inc(packed, 1)

            for b in range(2):
                turn(0, b)
            turn_and_project(1)
            with pe.Fori(2, LATE + 4) as g:
                turn_and_project(g)
            pe.wait_ge(const_done, 2)
            pe.wait_ge(bits_done, 1)
            pack(0, 0)
            for p in range(1, NT - 1):
                for g in range(2):
                    turn_and_project(LATE + 2 + 2 * p + g)
                pack(p, p)

            for b in range(2):
                project(T // 2 - 1, b)
            pack(NT - 1, NT - 1)

            def offsets(nb):
                wait(pe, cnt_ready, nb + 1)
                pe.matmul(off_ps, tri[:], cnt[:], start=True, stop=True).then_inc(off_done, 1)

            def expand(n, i):
                t = stage(n, i, 0)
                if t is not None:
                    wait(pe, r_s, 2 * t + 2)
                    wait(pe, einfo_ready, t)
                    for c in range(EC):
                        last = pe.matmul(info_ps[:, c, :], R[:, i, c * P:c * P + P],
                                         info[:, i, :], start=True, stop=True)
                    last.then_inc(info_e, 1)

            def slot(n, i):
                t = stage(n, i, DOT)
                if t is not None:
                    wait(pe, dot_s, 7 * t)
                    for c in range(EC):
                        last = pe.matmul(A_chunk(c), R[:, (i - DOT) % 4, c * P:c * P + P],
                                         Wh[:, bass.ds(t, 1), 0:D], start=True, stop=True)
                    last.then_inc(a_done, 1)
                if i == 1:
                    expand(n, 0)
                a = stage(n, i, FIND)
                if a is not None:
                    pack(a, i)
                t = stage(n, i, SUM)
                if t is not None:
                    b = (i - SUM) % 2
                    wait(pe, o_ready, t + 1)
                    wait(pe, dself_ready, t + 1)
                    wait(pe, y_ready, t - 1)
                    for c in range(EC):
                        pe.matmul(out_ps[b][:, 0:D + 1], O[:, b, c, :], G[:, (i - SUM) % 4, c, 0:D + 1],
                                  start=c == 0, stop=False)
                    pe.matmul(out_ps[b][:, 0:D + 1], dself[:, b, :], Wh[:, bass.ds(t, 1), 0:D + 1],
                              start=False, stop=True).then_inc(out_done, 1)
                if i == 0 and stage(n, i, 0) is not None:
                    offsets(n)
                if i > 0:
                    expand(n, i)

            slots(pe, slot)
            pe.wait_ge(flag_s, 3)
            pe.matmul(off_ps[:, 0:1], ones[:], flag_f[:, 2:3], start=True, stop=True).then_inc(flag_ps, 1)

            with pe.If(overflowed(pe)):
                def tile(t):
                    wait(pe, lw_turning, t + 1)
                    wait(pe, WhT_kept, t)
                    for k in range(K):
                        last = pe.transpose(turn_ps[:, k * P:k * P + P], lw[:, k * P:k * P + P], ident[:])
                    last.then_inc(lw_turned, 1)
                    wait(pe, diag_ready, t + 1)
                    wait(pe, nrow_kept, t)
                    pe.matmul(nrow_ps[:, 0:P], ones[:], diag, start=True, stop=True).then_inc(nrow_done, 1)

                tile(0)
                with pe.Fori(1, T) as t:
                    tile(t)

                def tile(t):
                    q = t * NCH
                    wait(pe, lw_ready, t + 1)
                    for c in range(NCH):
                        wait(pe, sim_ready, q + c)
                        for k in range(K):
                            last = pe.matmul(s_ps[:], lw[:, k * P:k * P + P], WhT[:, k, c * CH:c * CH + CH],
                                             start=k == 0, stop=k == K - 1)
                        last.then_inc(s_done, 1)
                        wait(pe, p_ready, q + c + 1)
                        wait(pe, pT_ready, q + c)
                        for b in range(B):
                            last = pe.transpose(pT_ps[:, b * P:b * P + P], pr[:, b * P:b * P + P], ident[:])
                        last.then_inc(pT_done, 1)
                        wait(pe, pT_ready, q + c + 1)
                        for b in range(B):
                            last = pe.matmul(pv_ps[:, 0:D + 1], pT[:, b * P:b * P + P], Wh[:, c * B + b, 0:D + 1],
                                             start=c == 0 and b == 0, stop=c == NCH - 1 and b == B - 1)
                        last.then_inc(pv_done, 1)

                tile(0)
                with pe.Fori(1, T) as t:
                    tile(t)

        QA = Q_ACT * WORDS

        @block.scalar
        def _(act):
            act.dma_start(adj_d[:], bass.AP(tensor=adj.tensor, offset=0, ap=[[N + 1, P], [P * (N + 1), T]]),
                          allow_slow_non_contiguous=True).then_inc(diag_loaded, 16)
            act.preload_act_table_set("sqrt_and_others")
            act.wait_ge(w_turned, 1)
            act.activation(WT[:], info_bank[:].rearrange("p (k d) -> p k d", k=K), ACT.Copy).then_inc(w_ready, 1)

            def keep(g):
                for b in range(2):
                    t = 2 * g + b
                    wait(act, wh_done, t + 1)
                    wait(act, wh_kept, t - 1)
                    act.activation(junk_a[:, b, :], out_ps[b][:, 0:D], ACT.Square, accum_out=nsq[:, bass.ds(t, 1)])
                    act.activation(Wh[:, bass.ds(t, 1), 0:D], out_ps[b][:, 0:D], ACT.Copy).then_inc(wh_kept, 1)

            def compare(a, j, lo=0, hi=QA):
                wait(act, adj_loaded[j], (a - j) * 4 + 16)
                wait(act, packed, a - 1)
                part = act.activation(mask[:, j % 2, lo:hi], adjb[:, j, lo:hi], ACT.Sign, bias=neg_half[:, 0:1])
                if hi == QA:
                    part.then_inc(mask_a, 1)

            def norms(q):
                act.wait_ge(wh_kept, q * XT + XT)
                act.activation(Wh[:, q * XT:q * XT + XT, D + 1], nsq[:, q * XT:q * XT + XT], ACT.Sqrt).then_inc(norm_kept, 1)

            keep(0)
            for q in range(LATE // XPAIRS):
                with act.Fori(max(1, q * XPAIRS), q * XPAIRS + XPAIRS) as g:
                    keep(g)
                norms(q)
            act.wait_ge(const_done, 2)
            for p in range(NT):
                for h in range(2):
                    g = LATE + 2 * p + h
                    keep(g)
                    compare(p, p, h * QA // 2, h * QA // 2 + QA // 2)
                    if g % XPAIRS == XPAIRS - 1:
                        norms(g // XPAIRS)
            act.preload_act_table_set("natural_log_exp_and_others")
            act.wait_ge(self_s, 4)
            act.activation(self_t[:], self_t[:], ACT.Exp).then_inc(self_e, 1)

            compare(NT, 0)

            def copy_info(n, i):
                t = stage(n, i, 0)
                if t is not None:
                    wait(act, info_e, t + 1)
                    wait(act, o_ready, t - 3)
                    act.activation(einfo[:, i, :, :], info_ps, ACT.Copy).then_inc(einfo_ready, 1)

            def slot(n, i):
                t_sum = stage(n, i, SUM)
                t_norm = stage(n, i, NORM)
                b_sum, b_norm = (i - SUM) % 2, (i - NORM) % 2
                if t_sum is not None:
                    wait(act, dot_s, 7 * t_sum + 7)
                    wait(act, o_ready, t_sum - 1)
                    act.activation(we[:, b_sum, :], sim[:, b_sum, :], ACT.Exp).then_inc(we_ready, 1)
                if t_norm is not None:
                    wait(act, rinv_ready, t_norm + 1)
                    wait(act, z_ready, t_norm - 1)
                    act.activation(ysb[:, b_norm, :], out_ps[b_norm][:, 0:D], ACT.Copy, scale=rinv[:, b_norm:b_norm + 1]).then_inc(y_ready, 1)
                if t_sum is not None:
                    wait(act, out_done, t_sum - 1)
                    act.activation(dself[:, b_sum, :], ident[:], ACT.Copy, scale=wself[:, bass.ds(t_sum, 1)]).then_inc(dself_ready, 1)
                if i == 1:
                    copy_info(n, 0)
                t = stage(n, i, OUT)
                if t is not None:
                    b = (i - OUT) % 2
                    wait(act, shift_ready, t + 1)
                    wait(act, stored[b], 16 * half(n, i, OUT))
                    act.activation(yo[:, b, :], z[:, b, :], ACT.Identity, scale=rstd[:, b:b + 1],
                                   bias=shift[:, b:b + 1]).then_inc(yo_ready, 1)
                a = stage(n, i, COMPARE)
                if a is not None:
                    compare(a, (i + 1) % NT)
                if i > 0:
                    copy_info(n, i)
                if t_norm is not None:
                    wait(act, bn_s, 2 * t_norm + 2)
                    act.activation(lnv[:, b_norm:b_norm + 1], mv[:, b_norm, 1:2], ACT.Ln, bias=ln_eps[:, 0:1]).then_inc(ln_s, 1)
                    wait(act, ln_s, 2 * t_norm + 1)
                    act.activation(rstd[:, b_norm:b_norm + 1], lnv[:, b_norm:b_norm + 1], ACT.Exp, scale=-0.5).then_inc(ln_s, 1)

            slots(act, slot)

            with act.If(overflowed(act)):
                def tile(t):
                    wait(act, lw_turned, t)
                    act.activation(lw, Wh[:, bass.ds(t, 1), 0:D].rearrange("p a d -> p (a d)"), ACT.Copy).then_inc(lw_turning, 1)
                    wait(act, lw_turned, t + 1)
                    act.activation(WhT[:, :, bass.ds(t * P, P)], turn_ps[:, 0:D].rearrange("p (k c) -> p k c", k=K),
                                   ACT.Copy).then_inc(WhT_kept, 1)

                tile(0)
                with act.Fori(1, T) as t:
                    tile(t)
                act.wait_ge(WhT_kept, T)
                act.wait_ge(nrow_kept, T)
                act.sem_inc(tile_free, 1)

                def tile(t):
                    q = t * NCH
                    wait(act, tile_free, t + 1)
                    act.activation(lw.rearrange("p (k c) -> p k c", k=K), WhT[:, :, bass.ds(t * P, P)], ACT.Copy).then_inc(lw_ready, 1)
                    for c in range(NCH):
                        wait(act, sim_ready, q + c + 1)
                        wait(act, p_ready, q + c)
                        act.activation(ex, sim_d, ACT.Exp).then_inc(ex_ready, 1)
                        wait(act, pT_done, q + c + 1)
                        wait(act, pv_done, q + c)
                        act.activation(pT, pT_ps[:], ACT.Copy).then_inc(pT_ready, 1)
                    wait(act, fin, 6 * t + 5)
                    act.activation(sm[:, 0:1], mv[:, 0, 1:2], ACT.Ln, bias=ln_eps[:, 0:1]).then_inc(lnv_d, 1)
                    wait(act, lnv_d, t + 1)
                    act.activation(sm[:, 1:2], sm[:, 0:1], ACT.Exp, scale=-0.5).then_inc(rstd_d, 1)
                    wait(act, fin, 6 * t + 6)
                    act.activation(yo[:, 0, :], z[:, 0, :], ACT.Identity, scale=sm[:, 1:2], bias=sm[:, 2:3]).then_inc(out_ready, 1)

                tile(0)
                with act.Fori(1, T) as t:
                    tile(t)

        @block.vector
        def _(dve):
            def compare(a, j):
                wait(dve, adj_loaded[j], (a - j) * 4 + 16)
                wait(dve, packed, a - 1)
                dve.tensor_scalar(mask[:, j % 2, QA:N], adjb[:, j, QA:N], 0.0, 0.5, ALU.is_gt, ALU.subtract).then_inc(mask_v, 1)

            def find(a, j, step):
                keys = pack_ps[j % 2][:, 0:WORDS]
                if step == 0:
                    wait_alone(dve, "dve", packed, a + 1)
                    dve.max(KK[:, j, 0:8], keys).then_inc(find_s, 1)
                if step == 1:
                    wait_alone(dve, "dve", find_s, 3 * a + 1)
                    dve.match_replace(out=keys_left[:], in_to_replace=KK[:, j, 0:8], in_values=keys, imm_value=0.0).then_inc(find_s, 1)
                if step == 2:
                    wait_alone(dve, "dve", find_s, 3 * a + 2)
                    dve.max(KK[:, j, 8:16], keys_left[:]).then_inc(find_s, 1)

            def hand(t, b):
                dve.tensor_copy(xs[:, b, :], X[:, bass.ds(t, 1), :].rearrange("p a d -> p (a d)")).then_inc(xs_ready, 1)

            def turned(g, more=True):
                for b in range(2):
                    t = 2 * g + b
                    wait(dve, x_turned, t + 1)
                    if more:
                        hand(t + 2, b)
                    wait(dve, wh_done, t - 1)
                    dve.tensor_copy(xT[:, b, :], a_ps[b][:, 0:D]).then_inc(xT_ready, 1)

            dve.wait_ge(x_loaded[0], 16)
            for b in range(2):
                hand(b, b)
            turned(0)
            for q in range(LATE // XPAIRS):
                with dve.Fori(max(1, q * XPAIRS), q * XPAIRS + XPAIRS - 1) as g:
                    turned(g)
                dve.wait_ge(x_loaded[q + 1], 16)
                turned(q * XPAIRS + XPAIRS - 1)
                if q == 0:
                    for w_q in range(BITS):
                        weight = float(2 ** (w_q + 7)) if w_q < Q_ACT else float(2 ** (w_q + 8))
                        last = dve.tensor_scalar(bit_w[:, w_q, :], ident[:], weight, None, ALU.mult)
                    last.then_inc(bits_done, 1)
                    dve.memset(info[:, :, 0:I_ROW], 0.0)
                    dve.memset(ov_k[:], 0.0)
                    dve.memset(ov_e[:], 0.0)
            for p in range(NT):
                for g in range(LATE + 2 * p, LATE + 2 * p + 2):
                    if g < T // 2 - 1 and (g + 1) % XPAIRS == 0:
                        dve.wait_ge(x_loaded[(g + 1) // XPAIRS], 16)
                    turned(g, g < T // 2 - 1)
                compare(p, p)
                if p > 0:
                    for k in range(3):
                        find(p - 1, p - 1, k)
            dve.wait_ge(norm_kept, XC)
            norm = Wh[:, :, D + 1]
            dve.tensor_tensor(self_t[:], norm, norm, ALU.mult).then_inc(self_s, 1)
            dve.wait_ge(self_s, 1)
            dve.tensor_scalar(self_t[:], self_t[:], SIM_EPS, None, ALU.add).then_inc(self_s, 1)
            dve.wait_ge(self_s, 2)
            dve.reciprocal(self_t[:], self_t[:]).then_inc(self_s, 1)
            dve.wait_ge(self_s, 3)
            dve.tensor_tensor(self_t[:], nsq[:], self_t[:], ALU.mult).then_inc(self_s, 1)
            dve.wait_ge(diag_loaded, 16)
            dve.wait_ge(self_e, 1)
            dve.scalar_tensor_tensor(out=wself[:], in0=adj_d[:], scalar=0.0, in1=self_t[:], op0=ALU.is_le,
                                     op1=ALU.mult).then_inc(self_s, 1)
            dve.wait_ge(self_s, 5)
            dve.tensor_scalar(wself[:], wself[:], TINY, None, ALU.max).then_inc(self_s, 1)

            B_OPS = 19
            count = [0]

            def batch(nb, part):
                s0 = B_OPS * nb

                def step(ins):
                    count[0] += 1
                    ins.then_inc(batch_s, 1)

                def settled(back=0, alone=False):
                    v = s0 + count[0] - back
                    (wait_alone(dve, "dve", batch_s, v) if alone else wait(dve, batch_s, v))

                def highest(level):
                    key = KK[:, :, level * K1:level * K1 + K1]
                    step(dve.tensor_scalar(key_p[:], key.bitcast(I32), EXP_BITS, None, ALU.bitwise_and))

                def without(level, rest):
                    step(dve.tensor_tensor(rest, KK[:, :, level * K1:level * K1 + K1], key_p[:].bitcast(F32), ALU.subtract))

                keys = KK[:, :, LIST:LIST + SLOTS]
                if part == 0:
                    count[0] = 0
                    wait(dve, find_s, 3 * (4 * nb + 4))
                    settled()
                    highest(0)
                if part == 1:
                    settled()
                    without(0, KK[:, :, K1:2 * K1])
                if part == 2:
                    settled()
                    highest(1)
                if part == 3:
                    settled()
                    without(1, KK[:, :, 2 * K1:3 * K1])
                if part == 4:
                    settled(alone=True)
                    for j in range(NT):
                        last = dve.max(KK[:, j, LIST + 8:LIST + 16], KK[:, j, 0:KEYS])
                    step(last)
                    highest(2)
                if part == 5:
                    settled()
                    without(2, key_r[:])
                    settled(1, alone=True)
                    for j in range(NT):
                        last = dve.match_replace(out=V_left[:, j, :], in_to_replace=KK[:, j, LIST + 8:LIST + 16],
                                                 in_values=KK[:, j, 0:KEYS], imm_value=0.0)
                    step(last)
                if part == 6:
                    settled(1)
                    step(dve.tensor_reduce(KK[:, :, LEFT], key_r[:], AX.X, ALU.max))
                    settled(1, alone=True)
                    for j in range(NT):
                        last = dve.max(KK[:, j, LIST:LIST + 8], V_left[:, j, :])
                    step(last)
                if part == 7:
                    settled()
                    step(dve.tensor_scalar(valid[:], keys, LO, None, ALU.is_ge))
                    step(dve.tensor_scalar(key_e[:], keys.bitcast(I32), 23, None, ALU.logical_shift_right))
                if part == 8:
                    settled(1)
                    if not isinstance(nb, int) or nb > 0:
                        wait(dve, off_done, nb)
                    dve.tensor_reduce(cnt[:], valid[:], AX.X, ALU.add).then_inc(cnt_ready, 1)
                    step(dve.tensor_copy(key_i[:], keys))
                    step(dve.tensor_tensor(ov_k[:], ov_k[:], KK[:, :, K1 - 1:LIST + 8:OV_STEP], ALU.max))
                if part == 9:
                    settled(1)
                    step(dve.tensor_scalar(key_i[:], key_i[:], 255, None, ALU.bitwise_and))
                    wait(dve, info_e, 4 * nb)
                    step(dve.tensor_copy(info[:, :, I_NORM], Wh[:, bass.ds(4 * nb, 4), D + 1]))
                    settled(1)
                    step(dve.scalar_tensor_tensor(out=info[:, :, 0:SLOTS], in0=key_e[:], scalar=256.0, in1=key_i[:],
                                                  op0=ALU.mult, op1=ALU.subtract))
                if part == 10:
                    wait(dve, off_done, nb + 1)
                    step(dve.tensor_copy(info[:, :, I_OFF], off_ps))
                    wait(dve, cnt_ready, nb + 1)
                    step(dve.tensor_tensor(info[:, :, I_END], off_ps, cnt[:], ALU.add))
                    settled()
                    dve.tensor_tensor(ov_e[:], ov_e[:], info[:, :, I_END], ALU.max).then_inc(info_ready, 1)
                    assert count[0] == B_OPS, count

            compare(NT, 0)
            for k in range(3):
                find(NT - 1, NT - 1, k)

            def slot(n, i):
                t_own, t_gather, t_dot, t_sum, t_norm, t_out = [stage(n, i, d) for d in (0, GATHER, DOT, SUM, NORM, OUT)]
                b_gather = (i - GATHER) % 4
                a_compare, a_find = stage(n, i, COMPARE), stage(n, i, FIND)
                ip = einfo[:, (i - GATHER) % 4, :, :]
                b_dot, g_dot = (i - DOT) % 2, (i - DOT) % 4
                b_sum, g_sum = (i - SUM) % 2, (i - SUM) % 4
                b_norm, b_out = (i - NORM) % 2, (i - OUT) % 2

                def product(c):
                    if t_dot is not None:
                        dve.tensor_tensor_reduce(junk[:, c, :], G[:, g_dot, c, 0:D], A_chunk(c), 1.0, 0.0, ALU.mult, ALU.add,
                                                 dot[:, c:c + 1]).then_inc(dot_s, 1)

                def lists(part):
                    if i == 0 and t_own is not None:
                        batch(n, part)

                def own(step):
                    if t_own is not None and step == 0:
                        wait(dve, info_ready, n + 1)
                        wait(dve, batch_s, B_OPS * (n + 1))
                        wait(dve, r_s, 2 * t_own)
                        dve.tensor_scalar(ge[:], edge_no[:], info[:, i, I_OFF:I_OFF + 1], None, ALU.is_ge).then_inc(r_s, 1)
                    if t_own is not None and step == 1:
                        wait(dve, r_s, 2 * t_own + 1)
                        wait(dve, a_done, t_own - 3)
                        dve.scalar_tensor_tensor(out=R[:, i, :], in0=edge_no[:], scalar=info[:, i, I_END:I_END + 1],
                                                 in1=ge[:], op0=ALU.is_lt, op1=ALU.mult).then_inc(r_s, 1)

                def other(step):
                    if t_gather is not None and step == 0:
                        wait(dve, einfo_ready, t_gather + 1)
                        wait(dve, j_s, 5 * t_gather)
                        dve.tensor_tensor(slot_e[:], edge_of[:], ip[:, :, I_OFF], ALU.subtract).then_inc(j_s, 1)
                    if t_gather is not None and step == 1:
                        wait(dve, j_s, 5 * t_gather + 1)
                        dve.tensor_tensor(hit[:], slot_no[:], slot_e[:].rearrange("p (c o) -> p c o", o=1).to_broadcast([P, EC, SLOTS]),
                                          ALU.is_equal).then_inc(j_s, 1)
                    if t_gather is not None and step == 2:
                        wait(dve, j_s, 5 * t_gather + 2)
                        dve.tensor_tensor(hitj[:], hit[:], ip[:, :, 0:SLOTS], ALU.mult).then_inc(j_s, 1)
                    if t_gather is not None and step == 3:
                        wait(dve, j_s, 5 * t_gather + 3)
                        dve.tensor_reduce(jf[:], hitj[:], AX.X, ALU.add).then_inc(j_s, 1)
                    if t_gather is not None and step == 4:
                        wait(dve, j_s, 5 * t_gather + 4)
                        wait(dve, gathered[b_gather], 48 * (n + (i - GATHER - b_gather) // 4))
                        dve.tensor_scalar(J[:, b_gather, :], jf[:], float(-J_SHIFT), None, ALU.add).then_inc(j_s, 1)

                def alike(step):
                    if t_dot is not None and step == 0:
                        wait(dve, a_done, t_dot + 1)
                        wait(dve, gathered[g_dot], 48 * (n + (i - DOT - g_dot) // 4 + 1))
                        wait(dve, einfo_ready, t_dot + 1)
                        wait(dve, dot_s, 7 * t_dot)
                        dve.tensor_tensor(nn[:], G[:, g_dot, :, D + 1], einfo[:, g_dot, :, I_NORM], ALU.mult).then_inc(dot_s, 1)
                    if t_dot is not None and step == 1:
                        wait(dve, dot_s, 7 * t_dot + 1)
                        dve.tensor_scalar(nn[:], nn[:], SIM_EPS, None, ALU.add).then_inc(dot_s, 1)
                    if t_dot is not None and step == 2:
                        wait(dve, dot_s, 7 * t_dot + 3)
                        dve.reciprocal(nn[:], nn[:]).then_inc(dot_s, 1)
                    if t_dot is not None and step == 3:
                        wait(dve, dot_s, 7 * t_dot + 6)
                        wait(dve, we_ready, t_dot - 1)
                        dve.tensor_tensor(sim[:, b_dot, :], dot[:], nn[:], ALU.mult).then_inc(dot_s, 1)

                def spread(step):
                    if t_norm is not None and step == 0:
                        wait(dve, z_ready, t_norm + 1)
                        wait(dve, bn_s, 2 * t_norm)
                        dve.bn_stats(st[:], z[:, b_norm, :]).then_inc(bn_s, 1)
                    if t_norm is not None and step == 1:
                        wait_alone(dve, "dve", bn_s, 2 * t_norm + 1)
                        wait_alone(dve, "dve", yo_ready, t_norm - 1)
                        dve.bn_aggr(mv[:, b_norm, :], st[:]).then_inc(bn_s, 1)

                def weigh(c):
                    if t_sum is not None:
                        wait(dve, we_ready, t_sum + 1)
                        wait(dve, out_done, t_sum - 1)
                        last = dve.tensor_scalar(O[:, b_sum, c, :], row1_no[:], einfo[:, g_sum, c, I_ROW:I_ROW + 1], we[:, b_sum, c:c + 1],
                                                 ALU.is_equal, ALU.mult)
                        if c == EC - 1:
                            last.then_inc(o_ready, 1)

                def finding(step):
                    if a_find is not None:
                        find(a_find, i, step)

                if t_norm is not None:
                    wait(dve, out_done, t_norm + 1)
                    wait(dve, y_ready, t_norm - 1)
                    dve.reciprocal(rinv[:, b_norm:b_norm + 1], out_ps[b_norm][:, D:D + 1]).then_inc(rinv_ready, 1)
                if i != 1:
                    other(0)
                lists(0)
                if i != 1:
                    other(1)
                lists(1)
                if i > 0:
                    own(0)
                if a_compare is not None:
                    compare(a_compare, (i + 1) % NT)
                weigh(0)
                if i != 1:
                    other(2)
                if t_out is not None:
                    wait(dve, ln_s, 2 * t_out + 2)
                    wait(dve, yo_ready, t_out - 1)
                    dve.scalar_tensor_tensor(out=shift[:, b_out:b_out + 1], in0=mv[:, b_out, 0:1], scalar=-1.0, in1=rstd[:, b_out:b_out + 1],
                                             op0=ALU.mult, op1=ALU.mult).then_inc(shift_ready, 1)
                lists(2)
                weigh(1)
                if i != 1:
                    other(3)
                lists(3)
                weigh(2)
                if i != 1:
                    other(4)
                lists(4)
                if i > 0:
                    own(1)
                if i == 1:
                    other(0)
                lists(5)
                alike(0)
                product(0)
                if i == 1:
                    other(1)
                lists(6)
                alike(1)
                if i == 1:
                    other(2)
                product(1)
                if i == 1:
                    other(3)
                lists(7)
                if i > 0:
                    finding(0)
                lists(8)
                alike(2)
                if i == 1:
                    other(4)
                lists(9)
                product(2)
                if i > 0:
                    finding(1)
                    spread(0)
                    alike(3)
                    finding(2)
                    spread(1)
                if i == 0:
                    spread(0)
                    lists(10)
                    alike(3)
                    own(0)
                    finding(0)
                    own(1)
                    finding(1)
                    spread(1)
                    finding(2)

            slots(dve, slot)
            dve.tensor_reduce(flag_f[:, 0:1], ov_k[:], AX.XY, ALU.max)
            dve.tensor_reduce(flag_f[:, 1:2], ov_e[:], AX.X, ALU.max).then_inc(flag_s, 1)
            dve.wait_ge(flag_s, 1)
            dve.tensor_scalar(flag_f[:, 0:1], flag_f[:, 0:1], LO, None, ALU.is_ge).then_inc(flag_s, 1)
            dve.wait_ge(flag_s, 2)
            dve.scalar_tensor_tensor(out=flag_f[:, 2:3], in0=flag_f[:, 1:2], scalar=float(EDGES), in1=flag_f[:, 0:1],
                                     op0=ALU.is_gt, op1=ALU.add).then_inc(flag_s, 1)
            dve.wait_ge(flag_ps, 1)
            dve.tensor_scalar(flag[:], off_ps[:, 0:1], 0.0, None, ALU.is_gt).then_inc(flag_ready, 1)

            with dve.If(overflowed(dve)):
                def tile(t):
                    wait(dve, nrow_done, t)
                    dve.tensor_scalar(diag, ident[:], Wh[:, bass.ds(t, 1), D + 1:D + 2].rearrange("p a b -> p (a b)"),
                                      None, ALU.mult).then_inc(diag_ready, 1)
                    wait(dve, nrow_done, t + 1)
                    dve.tensor_copy(norm_row[:, bass.ds(t * P, P)], nrow_ps[:, 0:P]).then_inc(nrow_kept, 1)

                tile(0)
                with dve.Fori(1, T) as t:
                    tile(t)
                dve.wait_ge(nrow_kept, T)
                dve.wait_ge(WhT_kept, T)
                def tile(t):
                    q = t * NCH
                    ni = Wh[:, bass.ds(t, 1), D + 1:D + 2].rearrange("p a b -> p (a b)")
                    own = adj_row[:, bass.ds(t * P, P)]
                    wait(dve, tile_free, t + 1)
                    wait(dve, row_loaded, 16 * t + 16)
                    dve.tensor_tensor(own, own, ident[:], ALU.max).then_inc(diag_set, 1)
                    wait(dve, diag_set, t + 1)
                    for c in range(NCH):
                        cs = slice(c * CH, c * CH + CH)
                        wait(dve, sim_ready, q + c)
                        dve.tensor_scalar(den, norm_row[:, cs], ni, SIM_EPS, ALU.mult, ALU.add).then_inc(den_ready, 1)
                        wait(dve, den_ready, q + c + 1)
                        dve.reciprocal(rec, den).then_inc(rec_ready, 1)
                        wait(dve, rec_ready, q + c + 1)
                        wait(dve, s_done, q + c + 1)
                        wait(dve, ex_ready, q + c)
                        dve.tensor_tensor(sim_d, s_ps[:], rec, ALU.mult).then_inc(sim_ready, 1)
                        wait(dve, ex_ready, q + c + 1)
                        wait(dve, pT_done, q + c)
                        dve.scalar_tensor_tensor(out=pr, in0=adj_row[:, cs], scalar=0.0, in1=ex, op0=ALU.is_gt,
                                                 op1=ALU.mult).then_inc(p_ready, 1)
                    e = 6 * t
                    wait(dve, pv_done, q + NCH)
                    dve.reciprocal(sm[:, 3:4], pv_ps[:, D:D + 1]).then_inc(fin, 1)
                    wait(dve, fin, e + 1)
                    dve.tensor_scalar(ysb[:, 0, :], pv_ps[:, 0:D], sm[:, 3:4], None, ALU.mult).then_inc(fin, 1)
                    wait(dve, fin, e + 2)
                    dve.tensor_tensor(z[:, 0, :], ysb[:, 0, :], X[:, bass.ds(t, 1), :].rearrange("p a b -> p (a b)"),
                                      ALU.add).then_inc(fin, 1)
                    wait(dve, fin, e + 3)
                    dve.bn_stats(st[:], z[:, 0, :]).then_inc(fin, 1)
                    wait_alone(dve, "dve", fin, e + 4)
                    dve.bn_aggr(mv[:, 0, :], st[:]).then_inc(fin, 1)
                    wait(dve, fin, e + 5)
                    wait(dve, rstd_d, t + 1)
                    dve.scalar_tensor_tensor(out=sm[:, 2:3], in0=mv[:, 0, 0:1], scalar=-1.0, in1=sm[:, 1:2],
                                             op0=ALU.mult, op1=ALU.mult).then_inc(fin, 1)

                tile(0)
                with dve.Fori(1, T) as t:
                    tile(t)


_INS = ["x", "adj", "L0_gnn_W"]


def kernel(**inputs):
    import numpy as _np
    import concourse.bacc as _bacc
    from concourse import mybir as _mybir
    from concourse.bass_utils import run_bass_kernel_spmd as _run

    nc = _bacc.Bacc("TRN2", target_bir_lowering=False, num_devices=1)
    arrays, args = {}, []
    for name in _INS:
        a = _np.ascontiguousarray(inputs[name])
        arrays[f"in_{name}"] = a
        args.append(nc.dram_tensor(f"in_{name}", a.shape, _mybir.dt.from_np(a.dtype), kind="ExternalInput").ap())
    o = nc.dram_tensor("out_0", inputs["x"].shape, _mybir.dt.float32, kind="ExternalOutput").ap()
    gnn_layer(nc, *args, o)
    r = _run(nc, [arrays], core_ids=[0])
    return r.results[0]["out_0"]
```
